# Optimizing a Trainium2 kernel written in Bass

```python
import numpy as np
import jax
import jax.numpy as jnp

def _softmax(x, axis=-1):
    return jax.nn.softmax(x, axis=axis)

def _gelu(x):
    return jax.nn.gelu(x, approximate=True)

def _silu(x):
    return jax.nn.silu(x)

def _sigmoid(x):
    return jax.nn.sigmoid(x)

def _layernorm(x, axis=-1, eps=1e-05):
    m = jnp.mean(x, axis=axis, keepdims=True)
    v = jnp.var(x, axis=axis, keepdims=True)
    return (x - m) / jnp.sqrt(v + eps)

def _scatter_add(tgt, idx, src, axis=0):
    return tgt.at[idx].add(src)

def _segment_sum(src, seg, n):
    return jax.ops.segment_sum(src, seg, n)
kernel_name = 'mk_adj_resnorm_d4_adj_r2_b6daa0'

def setup_inputs(seed: int=0):
    np.random.seed(seed)
    _w = jnp.asarray

    def _rec_inputs():
        import jax
        import jax.numpy as jnp
        _gk = jax.random.key(seed)
        x = -0.0005963 + 1.001 * jax.random.normal(jax.random.fold_in(_gk, 1), (32, 256, 384), jnp.float32)
        _a = jax.random.bernoulli(jax.random.fold_in(_gk, 2), 0.015625, (32, 256, 256))
        _a = jnp.logical_or(_a, jnp.swapaxes(_a, -1, -2))
        _a = jnp.logical_or(_a, jnp.eye(256, dtype=bool))
        adj = _a
        return (x, adj)
    x, adj = _rec_inputs()

    def _L0_gnn_setup():
        import jax, jax.numpy as jnp
        import numpy as np
        ATT_HEAD = 12
        IN_DIM = 384
        OUT_DIM = IN_DIM // ATT_HEAD
        LEAKY_ALPHA = 0.2
        B, N = (8, 256)
        key = jax.random.key(seed)
        ks = jax.random.split(key, 8)
        feat_in = jax.random.normal(ks[0], (B, N, IN_DIM), dtype=jnp.float32)
        adj = jax.random.randint(ks[1], (B, N, N), 0, 2) > 0
        lim_W = float(np.sqrt(6.0 / (IN_DIM + OUT_DIM)))
        W = jax.random.uniform(ks[2], (ATT_HEAD, IN_DIM, OUT_DIM), minval=-lim_W, maxval=lim_W, dtype=jnp.float32)
        b = jnp.zeros((OUT_DIM,), dtype=jnp.float32)
        lim_w = float(np.sqrt(6.0 / (OUT_DIM + 1)))
        w_src = jax.random.uniform(ks[3], (ATT_HEAD, OUT_DIM, 1), minval=-lim_w, maxval=lim_w, dtype=jnp.float32)
        w_dst = jax.random.uniform(ks[4], (ATT_HEAD, OUT_DIM, 1), minval=-lim_w, maxval=lim_w, dtype=jnp.float32)
        std_H = float(np.sqrt(2.0 / (IN_DIM + IN_DIM)))
        H_w = jax.random.normal(ks[5], (IN_DIM, IN_DIM), dtype=jnp.float32) * std_H
        H_b = jax.random.normal(ks[6], (IN_DIM,), dtype=jnp.float32) * 0.01
        return {'feat_in': feat_in, 'adj': adj, 'W': W, 'b': b, 'w_src': w_src, 'w_dst': w_dst, 'H_w': H_w, 'H_b': H_b}
    _L0_gnn_all = _L0_gnn_setup()
    _L0_gnn_in = {k: v for k, v in _L0_gnn_all.items() if k in ('W', 'b', 'w_src', 'w_dst', 'H_w', 'H_b')}
    del _L0_gnn_all

    def _L1_gnn_setup():
        import jax, jax.numpy as jnp
        import numpy as np
        B, S, H = (4, 1024, 384)
        NUM_HEADS = 6
        HEAD_SIZE = H // NUM_HEADS
        NEG = -9000000000000000.0

        def _heads(x):
            b, s, _ = x.shape
            return x.reshape(b, s, NUM_HEADS, HEAD_SIZE).transpose(0, 2, 1, 3)
        key = jax.random.key(seed)
        ks = jax.random.split(key, 10)
        seq_inputs = jax.random.normal(ks[0], (B, S, H), dtype=jnp.float32)
        gm = jax.random.randint(ks[1], (B, S, S), 0, 2) > 0
        graph_mask = gm | jnp.eye(S, dtype=bool)[None]
        sc = 1.0 / np.sqrt(H)
        Wq = jax.random.normal(ks[2], (H, H), dtype=jnp.float32) * sc
        bq = jnp.zeros((H,), dtype=jnp.float32)
        Wk = jax.random.normal(ks[3], (H, H), dtype=jnp.float32) * sc
        bk = jnp.zeros((H,), dtype=jnp.float32)
        Wv = jax.random.normal(ks[4], (H, H), dtype=jnp.float32) * sc
        bv = jnp.zeros((H,), dtype=jnp.float32)
        Wf = jax.random.normal(ks[5], (H, H), dtype=jnp.float32) * sc
        bf = jnp.zeros((H,), dtype=jnp.float32)
        return {'seq_inputs': seq_inputs, 'Wq': Wq, 'bq': bq, 'Wk': Wk, 'bk': bk, 'Wv': Wv, 'bv': bv, 'Wf': Wf, 'bf': bf, 'graph_mask': graph_mask}
    _L1_gnn_all = _L1_gnn_setup()
    _L1_gnn_in = {k: v for k, v in _L1_gnn_all.items() if k in ('Wq', 'bq', 'Wk', 'bk', 'Wv', 'bv', 'Wf', 'bf')}
    del _L1_gnn_all

    def _L2_gnn_setup():
        import jax, jax.numpy as jnp
        import numpy as np
        B, S, H = (4, 1024, 384)
        NUM_HEADS = 6
        HEAD_SIZE = H // NUM_HEADS
        NEG = -9000000000000000.0

        def _heads(x):
            b, s, _ = x.shape
            return x.reshape(b, s, NUM_HEADS, HEAD_SIZE).transpose(0, 2, 1, 3)
        key = jax.random.key(seed)
        ks = jax.random.split(key, 10)
        seq_inputs = jax.random.normal(ks[0], (B, S, H), dtype=jnp.float32)
        gm = jax.random.randint(ks[1], (B, S, S), 0, 2) > 0
        graph_mask = gm | jnp.eye(S, dtype=bool)[None]
        sc = 1.0 / np.sqrt(H)
        Wq = jax.random.normal(ks[2], (H, H), dtype=jnp.float32) * sc
        bq = jnp.zeros((H,), dtype=jnp.float32)
        Wk = jax.random.normal(ks[3], (H, H), dtype=jnp.float32) * sc
        bk = jnp.zeros((H,), dtype=jnp.float32)
        Wv = jax.random.normal(ks[4], (H, H), dtype=jnp.float32) * sc
        bv = jnp.zeros((H,), dtype=jnp.float32)
        Wf = jax.random.normal(ks[5], (H, H), dtype=jnp.float32) * sc
        bf = jnp.zeros((H,), dtype=jnp.float32)
        return {'seq_inputs': seq_inputs, 'Wq': Wq, 'bq': bq, 'Wk': Wk, 'bk': bk, 'Wv': Wv, 'bv': bv, 'Wf': Wf, 'bf': bf, 'graph_mask': graph_mask}
    _L2_gnn_all = _L2_gnn_setup()
    _L2_gnn_in = {k: v for k, v in _L2_gnn_all.items() if k in ('Wq', 'bq', 'Wk', 'bk', 'Wv', 'bv', 'Wf', 'bf')}
    del _L2_gnn_all

    def _L3_gnn_setup():
        import jax, jax.numpy as jnp
        import numpy as np
        B, S, H = (4, 1024, 384)
        NUM_HEADS = 6
        HEAD_SIZE = H // NUM_HEADS
        NEG = -9000000000000000.0

        def _heads(x):
            b, s, _ = x.shape
            return x.reshape(b, s, NUM_HEADS, HEAD_SIZE).transpose(0, 2, 1, 3)
        key = jax.random.key(seed)
        ks = jax.random.split(key, 10)
        seq_inputs = jax.random.normal(ks[0], (B, S, H), dtype=jnp.float32)
        gm = jax.random.randint(ks[1], (B, S, S), 0, 2) > 0
        graph_mask = gm | jnp.eye(S, dtype=bool)[None]
        sc = 1.0 / np.sqrt(H)
        Wq = jax.random.normal(ks[2], (H, H), dtype=jnp.float32) * sc
        bq = jnp.zeros((H,), dtype=jnp.float32)
        Wk = jax.random.normal(ks[3], (H, H), dtype=jnp.float32) * sc
        bk = jnp.zeros((H,), dtype=jnp.float32)
        Wv = jax.random.normal(ks[4], (H, H), dtype=jnp.float32) * sc
        bv = jnp.zeros((H,), dtype=jnp.float32)
        Wf = jax.random.normal(ks[5], (H, H), dtype=jnp.float32) * sc
        bf = jnp.zeros((H,), dtype=jnp.float32)
        return {'seq_inputs': seq_inputs, 'Wq': Wq, 'bq': bq, 'Wk': Wk, 'bk': bk, 'Wv': Wv, 'bv': bv, 'Wf': Wf, 'bf': bf, 'graph_mask': graph_mask}
    _L3_gnn_all = _L3_gnn_setup()
    _L3_gnn_in = {k: v for k, v in _L3_gnn_all.items() if k in ('Wq', 'bq', 'Wk', 'bk', 'Wv', 'bv', 'Wf', 'bf')}
    del _L3_gnn_all
    return {'x': x, 'adj': adj, 'L0_gnn_W': _L0_gnn_in['W'], 'L0_gnn_b': _L0_gnn_in['b'], 'L0_gnn_w_src': _L0_gnn_in['w_src'], 'L0_gnn_w_dst': _L0_gnn_in['w_dst'], 'L0_gnn_H_w': _L0_gnn_in['H_w'], 'L0_gnn_H_b': _L0_gnn_in['H_b'], 'L1_gnn_Wq': _L1_gnn_in['Wq'], 'L1_gnn_bq': _L1_gnn_in['bq'], 'L1_gnn_Wk': _L1_gnn_in['Wk'], 'L1_gnn_bk': _L1_gnn_in['bk'], 'L1_gnn_Wv': _L1_gnn_in['Wv'], 'L1_gnn_bv': _L1_gnn_in['bv'], 'L1_gnn_Wf': _L1_gnn_in['Wf'], 'L1_gnn_bf': _L1_gnn_in['bf'], 'L2_gnn_Wq': _L2_gnn_in['Wq'], 'L2_gnn_bq': _L2_gnn_in['bq'], 'L2_gnn_Wk': _L2_gnn_in['Wk'], 'L2_gnn_bk': _L2_gnn_in['bk'], 'L2_gnn_Wv': _L2_gnn_in['Wv'], 'L2_gnn_bv': _L2_gnn_in['bv'], 'L2_gnn_Wf': _L2_gnn_in['Wf'], 'L2_gnn_bf': _L2_gnn_in['bf'], 'L3_gnn_Wq': _L3_gnn_in['Wq'], 'L3_gnn_bq': _L3_gnn_in['bq'], 'L3_gnn_Wk': _L3_gnn_in['Wk'], 'L3_gnn_bk': _L3_gnn_in['bk'], 'L3_gnn_Wv': _L3_gnn_in['Wv'], 'L3_gnn_bv': _L3_gnn_in['bv'], 'L3_gnn_Wf': _L3_gnn_in['Wf'], 'L3_gnn_bf': _L3_gnn_in['bf']}

def reference(x, adj, L0_gnn_W, L0_gnn_b, L0_gnn_w_src, L0_gnn_w_dst, L0_gnn_H_w, L0_gnn_H_b, L1_gnn_Wq, L1_gnn_bq, L1_gnn_Wk, L1_gnn_bk, L1_gnn_Wv, L1_gnn_bv, L1_gnn_Wf, L1_gnn_bf, L2_gnn_Wq, L2_gnn_bq, L2_gnn_Wk, L2_gnn_bk, L2_gnn_Wv, L2_gnn_bv, L2_gnn_Wf, L2_gnn_bf, L3_gnn_Wq, L3_gnn_bq, L3_gnn_Wk, L3_gnn_bk, L3_gnn_Wv, L3_gnn_bv, L3_gnn_Wf, L3_gnn_bf):
    import jax
    import jax.numpy as jnp

    def _L0_gnn_ref(feat_in, adj, W, b, w_src, w_dst, H_w, H_b):
        import jax, jax.numpy as jnp
        import numpy as np
        ATT_HEAD = 12
        IN_DIM = 384
        OUT_DIM = IN_DIM // ATT_HEAD
        LEAKY_ALPHA = 0.2
        B, N = (8, 256)
        h = jnp.einsum('bnd,ade->bane', feat_in, W)
        th = jnp.tanh(h)
        attn_src = jnp.einsum('bane,aeo->bano', th, w_src)
        attn_dst = jnp.einsum('bane,aeo->bano', th, w_dst)
        attn = attn_src + jnp.swapaxes(attn_dst, 2, 3)
        attn = jnp.where(attn >= 0, attn, LEAKY_ALPHA * attn)
        mask = ~adj[:, None, :, :]
        attn = jnp.where(mask, jnp.float32(-999.0), attn)
        attn = jax.nn.softmax(attn, axis=-1)
        feat_out = jnp.einsum('banm,bame->bane', attn, h) + b
        feat_out = jnp.swapaxes(feat_out, 1, 2).reshape(feat_in.shape[0], feat_in.shape[1], -1)
        feat_out = jax.nn.elu(feat_out)
        gate = jax.nn.sigmoid(feat_in @ H_w.T + H_b)
        return gate * feat_out + (1.0 - gate) * feat_in

    def _L1_gnn_ref(seq_inputs, Wq, bq, Wk, bk, Wv, bv, Wf, bf, graph_mask):
        import jax, jax.numpy as jnp
        import numpy as np
        B, S, H = (4, 1024, 384)
        NUM_HEADS = 6
        HEAD_SIZE = H // NUM_HEADS
        NEG = -9000000000000000.0

        def _heads(x):
            b, s, _ = x.shape
            return x.reshape(b, s, NUM_HEADS, HEAD_SIZE).transpose(0, 2, 1, 3)
        q = _heads(seq_inputs @ Wq + bq)
        k = _heads(seq_inputs @ Wk + bk)
        v = _heads(seq_inputs @ Wv + bv)
        scores = jnp.einsum('bhqd,bhkd->bhqk', q, k) / np.sqrt(HEAD_SIZE)
        bias = jnp.where(graph_mask, 0.0, NEG)[:, None]
        probs = jax.nn.softmax(scores + bias, axis=-1)
        ctx = jnp.einsum('bhqk,bhkd->bhqd', probs, v)
        ctx = ctx.transpose(0, 2, 1, 3).reshape(seq_inputs.shape[0], seq_inputs.shape[1], H)
        return ctx @ Wf + bf

    def _L2_gnn_ref(seq_inputs, Wq, bq, Wk, bk, Wv, bv, Wf, bf, graph_mask):
        import jax, jax.numpy as jnp
        import numpy as np
        B, S, H = (4, 1024, 384)
        NUM_HEADS = 6
        HEAD_SIZE = H // NUM_HEADS
        NEG = -9000000000000000.0

        def _heads(x):
            b, s, _ = x.shape
            return x.reshape(b, s, NUM_HEADS, HEAD_SIZE).transpose(0, 2, 1, 3)
        q = _heads(seq_inputs @ Wq + bq)
        k = _heads(seq_inputs @ Wk + bk)
        v = _heads(seq_inputs @ Wv + bv)
        scores = jnp.einsum('bhqd,bhkd->bhqk', q, k) / np.sqrt(HEAD_SIZE)
        bias = jnp.where(graph_mask, 0.0, NEG)[:, None]
        probs = jax.nn.softmax(scores + bias, axis=-1)
        ctx = jnp.einsum('bhqk,bhkd->bhqd', probs, v)
        ctx = ctx.transpose(0, 2, 1, 3).reshape(seq_inputs.shape[0], seq_inputs.shape[1], H)
        return ctx @ Wf + bf

    def _L3_gnn_ref(seq_inputs, Wq, bq, Wk, bk, Wv, bv, Wf, bf, graph_mask):
        import jax, jax.numpy as jnp
        import numpy as np
        B, S, H = (4, 1024, 384)
        NUM_HEADS = 6
        HEAD_SIZE = H // NUM_HEADS
        NEG = -9000000000000000.0

        def _heads(x):
            b, s, _ = x.shape
            return x.reshape(b, s, NUM_HEADS, HEAD_SIZE).transpose(0, 2, 1, 3)
        q = _heads(seq_inputs @ Wq + bq)
        k = _heads(seq_inputs @ Wk + bk)
        v = _heads(seq_inputs @ Wv + bv)
        scores = jnp.einsum('bhqd,bhkd->bhqk', q, k) / np.sqrt(HEAD_SIZE)
        bias = jnp.where(graph_mask, 0.0, NEG)[:, None]
        probs = jax.nn.softmax(scores + bias, axis=-1)
        ctx = jnp.einsum('bhqk,bhkd->bhqd', probs, v)
        ctx = ctx.transpose(0, 2, 1, 3).reshape(seq_inputs.shape[0], seq_inputs.shape[1], H)
        return ctx @ Wf + bf
    x = _layernorm(x + _L0_gnn_ref(x, adj, L0_gnn_W, L0_gnn_b, L0_gnn_w_src, L0_gnn_w_dst, L0_gnn_H_w, L0_gnn_H_b), axis=-1)
    x = _layernorm(x + _L1_gnn_ref(x, L1_gnn_Wq, L1_gnn_bq, L1_gnn_Wk, L1_gnn_bk, L1_gnn_Wv, L1_gnn_bv, L1_gnn_Wf, L1_gnn_bf, adj), axis=-1)
    x = _layernorm(x + _L2_gnn_ref(x, L2_gnn_Wq, L2_gnn_bq, L2_gnn_Wk, L2_gnn_bk, L2_gnn_Wv, L2_gnn_bv, L2_gnn_Wf, L2_gnn_bf, adj), axis=-1)
    x = _layernorm(x + _L3_gnn_ref(x, L3_gnn_Wq, L3_gnn_bq, L3_gnn_Wk, L3_gnn_bk, L3_gnn_Wv, L3_gnn_bv, L3_gnn_Wf, L3_gnn_bf, adj), axis=-1)
    return x

_drawn_inputs = setup_inputs


def setup_inputs(seed=0):
    import zlib

    import numpy as np

    out = dict(_drawn_inputs(seed))
    spreads = {'L0_gnn_b': (0.0, 0.1),
     'L1_gnn_bq': (0.0, 0.1),
     'L1_gnn_bk': (0.0, 2.0),
     'L1_gnn_bv': (0.0, 0.1),
     'L1_gnn_bf': (0.0, 0.1),
     'L2_gnn_bq': (0.0, 0.321),
     'L2_gnn_bk': (0.0, 2.0),
     'L2_gnn_bv': (0.0, 0.1),
     'L2_gnn_bf': (0.0, 0.1),
     'L3_gnn_bq': (0.0, 0.33),
     'L3_gnn_bk': (0.0, 2.0),
     'L3_gnn_bv': (0.0, 0.1),
     'L3_gnn_bf': (0.0, 0.1)}
    factors = {'L0_gnn_H_b': 24.541}
    for name, (base, spread) in spreads.items():
        noise = np.random.default_rng([zlib.crc32(name.encode()), seed]).standard_normal(out[name].shape)
        drawn = base * np.exp(spread * noise) if base else spread * noise
        out[name] = jnp.asarray(drawn.astype(out[name].dtype))
    for name, factor in factors.items():
        out[name] = (out[name] * factor).astype(out[name].dtype)
    return out
```

```python
import concourse.bass as bass
from concourse import mybir
from contextlib import ExitStack

F32 = mybir.dt.float32
F32R = mybir.dt.float32r
BF16 = mybir.dt.bfloat16
U8 = mybir.dt.uint8
ALU = mybir.AluOpType
ACT = mybir.ActivationFunctionType

P = 128
B, N, D = 32, 256, 384
NT = N // P
DC = D // P
HALVES = B // 2
EPS = 1e-5

GAT_HEADS, GAT_DIM = 12, 32
HEADS, HEAD_DIM = 6, 64
LAYERS = 3

NEG = -9000000000000000.0
MASKED_GAT = -1e30
BIG = 3e38
CREDIT = NT


def at(per_unit, half, u, n):
    return half * (2 * per_unit) + (u * per_unit + n)


def f32(ap):
    return ap.bitcast(F32)


def held(eng, sem, value, passed):
    eng.wait_ge(sem, value)
    eng.sem_inc(passed, 1)


def product(pe, out, a, b, first=True, last=True):
    pe.matmul(out, a[1], b[0], start=first, stop=False)
    pe.matmul(out, a[0], b[1], start=False, stop=False)
    return pe.matmul(out, a[0], b[0], start=False, stop=last)


def gat_phase(nc, x, adj, y, w, w_sd, b_col, hb_row, ident_dram, sel_dram):
    STEPS = 9
    with ExitStack() as ctx:
        def sb(name, shape, dt=F32):
            return ctx.enter_context(nc.sbuf_tensor("g_" + name, shape, dt))

        def sem(name):
            return ctx.enter_context(nc.semaphore("g_" + name))

        x_sb = [sb(f"x{p}", [P, NT, D]) for p in range(2)]
        adj_sb = [sb(f"adj{p}", [P, NT, N], U8) for p in range(2)]
        mask = [sb(f"mask{p}", [P, NT, N], BF16) for p in range(2)]
        w_stage = sb("w_stage", [P, 2, DC, D])
        w_hi, w_lo = sb("w_hi", [P, 2, DC, D], F32R), sb("w_lo", [P, 2, DC, D], F32R)
        sd_stage = sb("sd_stage", [P, DC, P])
        sd_hi, sd_lo = sb("sd_hi", [P, DC, P], F32R), sb("sd_lo", [P, DC, P], F32R)
        b_sb = sb("b", [P, 1])
        hb_sb = sb("hb", [P, D])
        ident = sb("ident", [P, P])
        ident_bf = sb("ident_bf", [P, P], BF16)
        sel = sb("sel", [P, 2, GAT_HEADS])
        sel_dst = sb("sel_dst", [P, GAT_HEADS, P], F32R)
        sel_src = sb("sel_src", [P, GAT_HEADS, N], F32R)
        half_neg = sb("half_neg", [P, 1])
        xt_hi, xt_lo = sb("xt_hi", [P, DC, N], F32R), sb("xt_lo", [P, DC, N], F32R)
        th = sb("th", [P, NT, D])
        tt_hi, tt_lo = sb("tt_hi", [P, DC, N], F32R), sb("tt_lo", [P, DC, N], F32R)
        sd = [sb(f"sd{p}", [P, N], F32R) for p in range(2)]
        h_hi = [sb(f"h_hi{p}", [P, NT, GAT_HEADS, P], F32R) for p in range(2)]
        h_lo = [sb(f"h_lo{p}", [P, NT, GAT_HEADS, P], F32R) for p in range(2)]
        gate = [sb(f"gate{p}", [P, NT, D]) for p in range(2)]
        v_sb = sb("v", [P, 3, NT, N])
        probs = sb("probs", [P, 4, NT, N])
        nmax = sb("nmax", [P, 2, GAT_HEADS, NT])
        sums = sb("sums", [P, 2, GAT_HEADS, NT])
        recs = sb("recs", [P, 2, GAT_HEADS, NT])
        pt_hi, pt_lo = sb("pt_hi", [P, 2, NT, N], F32R), sb("pt_lo", [P, 2, NT, N], F32R)
        ct = sb("ct", [P, DC, N])
        ce = sb("ce", [P, DC, N])
        cx = sb("cx", [P, DC, N])
        mix = sb("mix", [P, NT, D])
        stats = sb("stats", [P, NT, 6])
        mv = sb("mv", [P, NT, 2])
        var = sb("var", [P, NT])
        rstd = sb("rstd", [P, NT])
        out_sb = [sb(f"out{p}", [P, NT, D]) for p in range(2)]
        z_ps = [ctx.enter_context(nc.psum_tensor(f"g_z{i}", [P, NT, N], F32)) for i in range(2)]
        pt_ps = [ctx.enter_context(nc.psum_tensor(f"g_pt{i}", [P, NT, N], F32)) for i in range(2)]
        cx_ps = [ctx.enter_context(nc.psum_tensor(f"g_cx{i}", [P, 512], F32)) for i in range(2)]
        pj_ps = [ctx.enter_context(nc.psum_tensor(f"g_pj{i}", [P, 512], F32)) for i in range(2)]

        passed = sem("passed")
        x_loaded = [sem(f"x_loaded{p}") for p in range(2)]
        stored = [sem(f"stored{p}") for p in range(2)]
        consts_loaded = sem("consts_loaded")
        consts_ready, zeros_ready, half_ready = sem("consts_ready"), sem("zeros_ready"), sem("half_ready")
        w_hi_done, w_split = sem("w_hi_done"), sem("w_split")
        mask_ready = sem("mask_ready")
        pj_made = sem("pj_made")
        pj_hi = sem("pj_hi")
        pj_read = sem("pj_read")
        back_made, back_read = sem("back_made"), sem("back_read")
        scores, lrelu, maxed = sem("scores"), sem("lrelu"), sem("maxed")
        exped, inverted, normed = sem("exped"), sem("inverted"), sem("normed")
        transposed, pt_hi_done, pt_split = sem("transposed"), sem("pt_hi_done"), sem("pt_split")
        contexts, ctx_read, ctx_min, ctx_exp, elu_done = (
            sem("contexts"), sem("ctx_read"), sem("ctx_min"), sem("ctx_exp"), sem("elu_done"))
        gate_exp, gate_add, gate_done = sem("gate_exp"), sem("gate_add"), sem("gate_done")
        gated, summed, bn, aggr = sem("gated"), sem("summed"), sem("bn"), sem("aggr")
        var_eps, rstd_done, ln_done = sem("var_eps"), sem("rstd_done"), sem("ln_done")

        X, H, TT, SD, G = 0, 2, 4, 6, 7
        HI_STEPS = SD + 1
        HEADS_J = GAT_HEADS + 4

        def step(half, u, k):
            return at(STEPS, half, u, k)

        def pj_bank(u, k):
            return pj_ps[(u + k) % 2]

        def rounds():
            plan = {0: [X], 1: [X + 1], 2: [H], 3: [H + 1], 6: [TT], 7: [TT + 1], 9: [SD]}
            return [(j, plan.get(j, [])) for j in range(HEADS_J)]

        block = ctx.enter_context(nc.Block())

        @block.sync
        def _(sp):
            def load(half, u):
                s = half * 2 + u
                sp.dma_start(x_sb[u][:, :, :], x[bass.ds(s, 1), :, :].rearrange("o (t p) d -> p (o t) d", p=P)).then_inc(x_loaded[u], 16)
                sp.dma_start(adj_sb[u][:, :, :], adj[bass.ds(s, 1), :, :].rearrange("o (t p) d -> p (o t) d", p=P)).then_inc(x_loaded[u], 16)

            def store(half, u):
                held(sp, ln_done, at(NT, half, u, NT), passed)
                sp.dma_start(y[bass.ds(half * 2 + u, 1), :, :].rearrange("o (t p) d -> p (o t) d", p=P), out_sb[u][:, :, :]).then_inc(stored[u], 16)

            load(0, 0)
            for tile, source in ((ident, ident_dram), (sel, sel_dram), (w_stage, w), (sd_stage, w_sd), (b_sb, b_col)):
                sp.dma_start(tile[:], source).then_inc(consts_loaded, 16)
            sp.dma_start(hb_sb[:, :], hb_row.partition_broadcast(P)).then_inc(consts_loaded, 16)
            load(0, 1)
            with sp.Fori(0, HALVES - 1) as half:
                for u in range(2):
                    held(sp, summed, at(NT, half, u, NT), passed)
                    load(half + 1, u)
                    store(half, u)
            for u in range(2):
                store(HALVES - 1, u)
            for u in range(2):
                sp.wait_ge(stored[u], 16 * HALVES)

        @block.gpsimd
        def _(pool):
            pool.memset(half_neg[:, :], -0.5).then_inc(half_ready, 1)
            for p in range(2):
                pool.memset(f32(h_hi[p][:, :, :, :]), 0.0).then_inc(zeros_ready, 1)
                pool.memset(f32(h_lo[p][:, :, :, :]), 0.0).then_inc(zeros_ready, 1)

            def make_mask(half, u):
                held(pool, x_loaded[u], half * 32 + 32, passed)
                pool.tensor_scalar(mask[u][:, :, :], adj_sb[u][:, :, :], -1.0, -MASKED_GAT, ALU.add, ALU.mult).then_inc(mask_ready, 1)

            def gate_plus_one(half, u, t):
                held(pool, gate_exp, at(NT, half, u, t + 1), passed)
                pool.tensor_scalar(gate[u][:, t, :], gate[u][:, t, :], 1.0, None, ALU.add).then_inc(gate_add, 1)

            def normalise(half, u, h):
                held(pool, inverted, at(GAT_HEADS, half, u, h + 1), passed)
                i = h % 4
                for t in range(NT):
                    last = pool.tensor_scalar(probs[:, i, t, :], probs[:, i, t, :], recs[:, u, h, t:t + 1], None, ALU.mult)
                last.then_inc(normed, 1)

            def context_min(half, u):
                held(pool, ctx_read, at(DC, half, u, DC), passed)
                pool.tensor_scalar(ce[:, :, :], ct[:, :, :], 0.0, None, ALU.min).then_inc(ctx_min, 1)

            def gate_times(half, u, t):
                pool.wait_ge(back_read, CREDIT + at(NT, half, u, t + 1))
                pool.tensor_tensor(mix[:, t, :], mix[:, t, :], gate[u][:, t, :], ALU.mult).then_inc(gated, 1)

            def inverse_std(half, u, t):
                held(pool, aggr, at(NT, half, u, t + 1), passed)
                pool.tensor_scalar(var[:, t:t + 1], mv[:, t, 1:2], EPS, None, ALU.add).then_inc(var_eps, 1)
                pool.wait_ge(var_eps, at(NT, half, u, t + 1))
                pool.tensor_tensor(rstd[:, t:t + 1], var[:, t:t + 1], half_neg[:, :], ALU.pow).then_inc(rstd_done, 1)

            def slot(half, u, nxt):
                for j, steps in rounds():
                    if nxt and j == 2:
                        make_mask(*nxt)
                    if 0 <= j - 2 < GAT_HEADS:
                        normalise(half, u, j - 2)
                context_min(half, u)
                if nxt:
                    for t in range(NT):
                        gate_plus_one(*nxt, t)
                for t in range(NT):
                    gate_times(half, u, t)
                for t in range(NT):
                    inverse_std(half, u, t)

            pool.wait_ge(half_ready, 1)
            make_mask(0, 0)
            for t in range(NT):
                gate_plus_one(0, 0, t)
            with pool.Fori(0, HALVES - 1) as half:
                slot(half, 0, (half, 1))
                slot(half, 1, (half + 1, 0))
            slot(HALVES - 1, 0, (HALVES - 1, 1))
            slot(HALVES - 1, 1, None)

        def padded(tile, t):
            g = tile[:, t, :, :].rearrange("p (c a) n -> p c (a n)", a=4)
            return [g[:, :, a * (P + GAT_DIM):a * (P + GAT_DIM) + GAT_DIM] for a in range(4)]

        @block.scalar
        def _(act):
            act.wait_ge(consts_loaded, 96)
            for m in range(2):
                act.activation(w_hi[:, m], w_stage[:, m], ACT.Identity).then_inc(w_hi_done, 1)
            act.activation(sd_hi[:, :, :], sd_stage[:, :, :], ACT.Identity).then_inc(w_hi_done, 1)
            act.wait_ge(zeros_ready, 4)

            def hi_of_step(half, u, k):
                ps = pj_bank(u, k)
                act.wait_ge(pj_made, step(half, u, k) + 1)
                if k in (X, X + 1):
                    t = k - X
                    act.activation(xt_hi[:, :, t * P:(t + 1) * P], ps[:, 0:D].rearrange("p (c n) -> p c n", c=DC), ACT.Identity).then_inc(pj_hi, 1)
                elif k in (H, H + 1):
                    t = k - H
                    act.activation(th[:, t, :], ps[:, 0:D], ACT.Tanh)
                    src = ps[:, 0:D].rearrange("p (c a e) -> p c a e", a=4, e=GAT_DIM)
                    for a, dst in enumerate(padded(h_hi[u], t)):
                        last = act.activation(dst, src[:, :, a, :], ACT.Identity)
                    last.then_inc(pj_hi, 1)
                elif k in (TT, TT + 1):
                    t = k - TT
                    act.activation(tt_hi[:, :, t * P:(t + 1) * P], ps[:, 0:D].rearrange("p (c n) -> p c n", c=DC), ACT.Identity).then_inc(pj_hi, 1)
                elif k == SD:
                    act.activation(sd[u][:, :], ps[:, 0:N], ACT.Identity).then_inc(pj_hi, 1)

            def gate_exponential(half, u, t):
                act.wait_ge(pj_read, step(half, u, G + t) + 1)
                act.activation(gate[u][:, t, :], gate[u][:, t, :], ACT.Exp, scale=-1.0).then_inc(gate_exp, 1)

            def slot(half, u, nxt):
                for j, steps in rounds():
                    if nxt:
                        for k in steps:
                            hi_of_step(*nxt, k)
                    if j < GAT_HEADS:
                        act.wait_ge(scores, at(GAT_HEADS, half, u, j + 1))
                        act.wait_ge(exped, at(GAT_HEADS, half, u, max(j - 2, 0)))
                        act.activation(v_sb[:, j % 3], z_ps[j % 2][:, :, :], ACT.Relu, scale=-0.8).then_inc(lrelu, 1)
                    if 0 <= j - 3 < GAT_HEADS:
                        h = j - 3
                        act.wait_ge(transposed, at(GAT_HEADS, half, u, h + 1))
                        act.wait_ge(contexts, at(GAT_HEADS, half, u, max(h - 1, 0)))
                        act.activation(pt_hi[:, h % 2], pt_ps[h % 2][:, :, :], ACT.Identity).then_inc(pt_hi_done, 1)
                    if 0 <= j - 1 < GAT_HEADS:
                        h = j - 1
                        act.wait_ge(maxed, at(GAT_HEADS, half, u, h + 1))
                        act.wait_ge(transposed, at(GAT_HEADS, half, u, max(h - 3, 0)))
                        for t in range(NT):
                            last = act.activation(probs[:, h % 4, t, :], v_sb[:, h % 3, t, :], ACT.Exp, scale=-1.0,
                                                  bias=nmax[:, u, h, t:t + 1], accum_out=sums[:, u, h, t:t + 1])
                        last.then_inc(exped, 1)
                    if 0 <= j - 4 < GAT_HEADS and (j - 4) % 4 == 3:
                        c = (j - 4) // 4
                        act.wait_ge(contexts, at(GAT_HEADS, half, u, 4 * c + 4))
                        act.wait_ge(elu_done, at(1, half, u, 0))
                        act.activation(ct[:, c, :], cx_ps[(3 * u + c) % 2][:, 0:N], ACT.Identity, bias=b_sb[:, 0:1]).then_inc(ctx_read, 1)
                act.wait_ge(ctx_min, at(1, half, u, 1))
                act.activation(ce[:, :, :], ce[:, :, :], ACT.Exp).then_inc(ctx_exp, 1)
                if nxt:
                    for t in range(NT):
                        gate_exponential(*nxt, t)

            for k in range(G):
                hi_of_step(0, 0, k)
            for t in range(NT):
                gate_exponential(0, 0, t)
            with act.Fori(0, HALVES - 1) as half:
                slot(half, 0, (half, 1))
                slot(half, 1, (half + 1, 0))
            slot(HALVES - 1, 0, (HALVES - 1, 1))
            slot(HALVES - 1, 1, None)

        @block.vector
        def _(dve):
            dve.sem_inc(back_read, CREDIT)
            dve.wait_ge(consts_loaded, 96)
            dve.tensor_copy(ident_bf[:, :], ident[:, :])
            dve.tensor_copy(sel_dst[:, :, :], sel[:, 0, :].unsqueeze(2).to_broadcast([P, GAT_HEADS, P]))
            dve.tensor_copy(sel_src[:, :, :], sel[:, 1, :].unsqueeze(2).to_broadcast([P, GAT_HEADS, N])).then_inc(consts_ready, 1)
            for m in range(2):
                dve.wait_ge(w_hi_done, m + 1)
                dve.tensor_tensor(w_lo[:, m], w_stage[:, m], f32(w_hi[:, m]), ALU.subtract).then_inc(w_split, 1)
            dve.wait_ge(w_hi_done, 3)
            dve.tensor_tensor(sd_lo[:, :, :], sd_stage[:, :, :], f32(sd_hi[:, :, :]), ALU.subtract).then_inc(w_split, 1)

            def lo_of_step(half, u, k):
                ps = pj_bank(u, k)
                if k in (G, G + 1):
                    t = k - G
                    dve.wait_ge(pj_made, step(half, u, k) + 1)
                    dve.tensor_tensor(gate[u][:, t, :], ps[:, 0:D], hb_sb[:, :], ALU.add).then_inc(pj_read, 1)
                    return
                dve.wait_ge(pj_hi, at(HI_STEPS, half, u, k) + 1)
                if k in (X, X + 1):
                    cols = slice((k - X) * P, (k - X + 1) * P)
                    dve.tensor_tensor(xt_lo[:, :, cols], ps[:, 0:D].rearrange("p (c n) -> p c n", c=DC), f32(xt_hi[:, :, cols]), ALU.subtract).then_inc(pj_read, 1)
                elif k in (H, H + 1):
                    t = k - H
                    src = ps[:, 0:D].rearrange("p (c a e) -> p c a e", a=4, e=GAT_DIM)
                    for a, (hi, lo) in enumerate(zip(padded(h_hi[u], t), padded(h_lo[u], t))):
                        last = dve.tensor_tensor(lo, src[:, :, a, :], f32(hi), ALU.subtract)
                    last.then_inc(pj_read, 1)
                elif k in (TT, TT + 1):
                    cols = slice((k - TT) * P, (k - TT + 1) * P)
                    dve.tensor_tensor(tt_lo[:, :, cols], ps[:, 0:D].rearrange("p (c n) -> p c n", c=DC), f32(tt_hi[:, :, cols]), ALU.subtract).then_inc(pj_read, 1)
                elif k == SD:
                    for q in (1, 3):
                        rows = slice(32 * q, 32 * q + 32)
                        last = dve.tensor_tensor(sd[u][rows, :], ps[rows, 0:N], f32(sd[u][rows, :]), ALU.subtract)
                    last.then_inc(pj_read, 1)

            def invert(half, u, h):
                dve.wait_ge(exped, at(GAT_HEADS, half, u, h + 1))
                dve.reciprocal(recs[:, u, h, :], sums[:, u, h, :]).then_inc(inverted, 1)

            def invert_gate(half, u, t):
                dve.wait_ge(gate_add, at(NT, half, u, t + 1))
                dve.reciprocal(gate[u][:, t, :], gate[u][:, t, :]).then_inc(gate_done, 1)

            def slot(half, u, nxt):
                for j, steps in rounds():
                    if 0 <= j - 2 < GAT_HEADS:
                        invert(half, u, j - 2)
                    if nxt:
                        for k in steps:
                            lo_of_step(*nxt, k)
                    if j < GAT_HEADS:
                        held(dve, lrelu, at(GAT_HEADS, half, u, j + 1), passed)
                        for t in range(NT):
                            last = dve.tensor_tensor_reduce(
                                out=v_sb[:, j % 3, t, :], in0=z_ps[j % 2][:, t, :], in1=v_sb[:, j % 3, t, :], scale=-1.0,
                                scalar=BIG, op0=ALU.add, op1=ALU.min, accum_out=nmax[:, u, j, t:t + 1])
                        last.then_inc(maxed, 1)
                    if 0 <= j - 3 < GAT_HEADS:
                        h = j - 3
                        dve.wait_ge(pt_hi_done, at(GAT_HEADS, half, u, h + 1))
                        dve.tensor_tensor(pt_lo[:, h % 2], pt_ps[h % 2][:, :, :], f32(pt_hi[:, h % 2]), ALU.subtract).then_inc(pt_split, 1)
                if nxt:
                    for k in (G, G + 1):
                        lo_of_step(*nxt, k)
                dve.wait_ge(ctx_exp, at(1, half, u, 1))
                dve.scalar_tensor_tensor(cx[:, :, :], ce[:, :, :], -1.0, ct[:, :, :], ALU.add, ALU.max).then_inc(elu_done, 1)
                if nxt:
                    for t in range(NT):
                        invert_gate(*nxt, t)
                for t in range(NT):
                    dve.wait_ge(back_made, at(NT, half, u, t + 1))
                    dve.tensor_tensor(mix[:, t, :], pj_bank(u, t)[:, 0:D], x_sb[u][:, t, :], ALU.subtract).then_inc(back_read, 1)
                for t in range(NT):
                    dve.wait_ge(gated, at(NT, half, u, t + 1))
                    dve.scalar_tensor_tensor(mix[:, t, :], x_sb[u][:, t, :], 2.0, mix[:, t, :], ALU.mult, ALU.add).then_inc(summed, 1)
                    dve.wait_ge(summed, at(NT, half, u, t + 1))
                    dve.bn_stats(stats[:, t, :], mix[:, t, :]).then_inc(bn, 1)
                    held(dve, bn, at(NT, half, u, t + 1), passed)
                    dve.bn_aggr(mv[:, t, :], stats[:, t, :]).then_inc(aggr, 1)
                dve.wait_ge(stored[u], half * 16)
                for t in range(NT):
                    dve.wait_ge(rstd_done, at(NT, half, u, t + 1))
                    dve.tensor_scalar(out_sb[u][:, t, :], mix[:, t, :], mv[:, t, 0:1], rstd[:, t:t + 1], ALU.subtract, ALU.mult).then_inc(ln_done, 1)

            for k in range(STEPS):
                lo_of_step(0, 0, k)
            for t in range(NT):
                invert_gate(0, 0, t)
            with dve.Fori(0, HALVES - 1) as half:
                slot(half, 0, (half, 1))
                slot(half, 1, (half + 1, 0))
            slot(HALVES - 1, 0, (HALVES - 1, 1))
            slot(HALVES - 1, 1, None)

        @block.tensor
        def _(pe):
            def make_step(half, u, k, begins=False):
                ps = pj_bank(u, k)
                n = step(half, u, k)
                if k >= H:
                    pe.wait_ge(pj_read, n if k in (H, SD) else n - 1)
                elif not begins:
                    pe.wait_ge(pj_read, n - 1)
                    pe.wait_ge(back_read, CREDIT + at(NT, half, u, k - 3))
                if k in (X, X + 1):
                    t = k - X
                    pe.wait_ge(x_loaded[u], half * 32 + 32)
                    for c in range(DC):
                        last = pe.transpose(ps[:, c * P:(c + 1) * P], x_sb[u][:, t, c * P:(c + 1) * P], ident[:, :])
                elif k in (H, H + 1, G, G + 1):
                    m = 0 if k in (H, H + 1) else 1
                    t = k - (H, G)[m]
                    rows = slice(t * P, (t + 1) * P)
                    for c in range(DC):
                        last = product(pe, ps[:, 0:D], (xt_hi[:, c, rows], xt_lo[:, c, rows]), (w_hi[:, m, c, :], w_lo[:, m, c, :]),
                                       first=c == 0, last=c == DC - 1)
                elif k in (TT, TT + 1):
                    t = k - TT
                    for c in range(DC):
                        last = pe.transpose(ps[:, c * P:(c + 1) * P], th[:, t, c * P:(c + 1) * P], ident[:, :])
                else:
                    for c in range(DC):
                        last = product(pe, ps[:, 0:N], (sd_hi[:, c, :], sd_lo[:, c, :]), (tt_hi[:, c, :], tt_lo[:, c, :]),
                                       first=c == 0, last=c == DC - 1)
                last.then_inc(pj_made, 1)

            def make_back(half, u, t, nxt):
                if t == 0:
                    pe.wait_ge(elu_done, at(1, half, u, 1))
                if nxt:
                    pe.wait_ge(pj_read, step(*nxt, STEPS - 1 + t))
                else:
                    pe.wait_ge(back_read, CREDIT + at(NT, half, u, 0))
                for c in range(DC):
                    last = pe.transpose(pj_bank(u, t)[:, c * P:(c + 1) * P], cx[:, c, t * P:(t + 1) * P], ident[:, :])
                last.then_inc(back_made, 1)

            def slot(half, u, nxt):
                for j, steps in rounds():
                    if j < GAT_HEADS:
                        if j == 0:
                            pe.wait_ge(pj_read, step(half, u, SD) + 1)
                            pe.wait_ge(mask_ready, at(1, half, u, 1))
                        pe.wait_ge(maxed, at(GAT_HEADS, half, u, max(j - 1, 0)))
                        for t in range(NT):
                            z = z_ps[j % 2][:, t, :]
                            pe.matmul(z, sel_dst[:, j, :], sd[u][:, :], start=True, stop=False)
                            pe.matmul(z, sd[u][:, t * P:(t + 1) * P], sel_src[:, j, :], start=False, stop=False)
                            last = pe.matmul(z, ident_bf[:, :], mask[u][:, t, :], start=False, stop=True)
                        last.then_inc(scores, 1)
                    if nxt:
                        for k in steps:
                            make_step(*nxt, k)
                    if 0 <= j - 3 < GAT_HEADS:
                        h = j - 3
                        pe.wait_ge(normed, at(GAT_HEADS, half, u, h + 1))
                        pe.wait_ge(pt_split, at(GAT_HEADS, half, u, max(h - 1, 0)))
                        for t in range(NT):
                            for kt in range(NT):
                                last = pe.transpose(pt_ps[h % 2][:, kt, t * P:(t + 1) * P], probs[:, h % 4, t, kt * P:(kt + 1) * P], ident[:, :])
                        last.then_inc(transposed, 1)
                    if 0 <= j - 4 < GAT_HEADS:
                        h = j - 4
                        c = h // 4
                        pe.wait_ge(pt_split, at(GAT_HEADS, half, u, h + 1))
                        if h % 4 == 0:
                            pe.wait_ge(ctx_read, at(DC, half, u, max(c - 1, 0)))
                        for kt in range(NT):
                            last = product(pe, cx_ps[(3 * u + c) % 2][:, 0:N], (h_hi[u][:, kt, h, :], h_lo[u][:, kt, h, :]),
                                           (pt_hi[:, h % 2, kt, :], pt_lo[:, h % 2, kt, :]),
                                           first=h % 4 == 0 and kt == 0, last=h % 4 == 3 and kt == NT - 1)
                        last.then_inc(contexts, 1)
                if nxt:
                    for k in (G, G + 1):
                        make_step(*nxt, k)
                for t in range(NT):
                    make_back(half, u, t, nxt)

            pe.wait_ge(consts_loaded, 96)
            pe.wait_ge(consts_ready, 1)
            for k in range(STEPS):
                if k == H:
                    pe.wait_ge(w_split, 3)
                make_step(0, 0, k, begins=True)
            with pe.Fori(0, HALVES - 1) as half:
                slot(half, 0, (half, 1))
                slot(half, 1, (half + 1, 0))
            slot(HALVES - 1, 0, (HALVES - 1, 1))
            slot(HALVES - 1, 1, None)


def attention_phase(nc, y, adj, w, b_col, b_row, ident_dram):
    STEPS = 7
    Q, K, V, O = range(4)
    with ExitStack() as ctx:
        def sb(name, shape, dt=F32):
            return ctx.enter_context(nc.sbuf_tensor("a_" + name, shape, dt))

        def sem(name):
            return ctx.enter_context(nc.semaphore("a_" + name))

        x_sb = [sb(f"x{p}", [P, NT, D]) for p in range(2)]
        adj_sb = [sb(f"adj{p}", [P, NT, N], U8) for p in range(2)]
        mask = [sb(f"mask{p}", [P, NT, N]) for p in range(2)]
        w_stage = sb("w_stage", [P, 4, DC, D])
        w_hi, w_lo = sb("w_hi", [P, 4, DC, D], F32R), sb("w_lo", [P, 4, DC, D], F32R)
        bc_stage, br_stage = sb("bc_stage", [P, 2, DC]), sb("br_stage", [P, 2, D])
        bc, br = sb("bc", [P, 2, DC]), sb("br", [P, 2, D])
        ident = sb("ident", [P, P])
        half_neg = sb("half_neg", [P, 1])
        xt_hi, xt_lo = sb("xt_hi", [P, DC, N], F32R), sb("xt_lo", [P, DC, N], F32R)
        qk_hi = [sb(f"qk_hi{p}", [P, DC, 2, N], F32R) for p in range(2)]
        qk_lo = [sb(f"qk_lo{p}", [P, DC, 2, N], F32R) for p in range(2)]
        v = sb("v", [P, NT, D])
        v_hi = [sb(f"v_hi{p}", [P, NT, HEADS, P], F32R) for p in range(2)]
        v_lo = [sb(f"v_lo{p}", [P, NT, HEADS, P], F32R) for p in range(2)]
        logits = sb("logits", [P, 2, NT, N])
        probs = sb("probs", [P, 4, NT, N])
        nmax = sb("nmax", [P, 2, HEADS, NT])
        sums = sb("sums", [P, 2, HEADS, NT])
        recs = sb("recs", [P, 2, HEADS, NT])
        pt_hi, pt_lo = sb("pt_hi", [P, 2, NT, N], F32R), sb("pt_lo", [P, 2, NT, N], F32R)
        ct_hi, ct_lo = sb("ct_hi", [P, DC, N], F32R), sb("ct_lo", [P, DC, N], F32R)
        mix = sb("mix", [P, NT, D])
        stats = sb("stats", [P, NT, 6])
        mv = sb("mv", [P, NT, 2])
        var = sb("var", [P, NT])
        rstd = sb("rstd", [P, NT])
        out_sb = [sb(f"out{p}", [P, NT, D]) for p in range(2)]
        s_ps = [ctx.enter_context(nc.psum_tensor(f"a_s{i}", [P, NT, N], F32)) for i in range(2)]
        pt_ps = [ctx.enter_context(nc.psum_tensor(f"a_pt{i}", [P, NT, N], F32)) for i in range(2)]
        cx_ps = [ctx.enter_context(nc.psum_tensor(f"a_cx{i}", [P, 512], F32)) for i in range(2)]
        pj_ps = [ctx.enter_context(nc.psum_tensor(f"a_pj{i}", [P, 512], F32)) for i in range(2)]

        passed = sem("passed")
        x_loaded = [sem(f"x_loaded{p}") for p in range(2)]
        stored = [sem(f"stored{p}") for p in range(2)]
        ident_loaded, w_loaded = sem("ident_loaded"), sem("w_loaded")
        half_ready, zeros_ready = sem("half_ready"), sem("zeros_ready")
        w_hi_done, w_split, b_ready = sem("w_hi_done"), sem("w_split"), sem("b_ready")
        mask_ready, x_biased = sem("mask_ready"), sem("x_biased")
        pj_made = sem("pj_made")
        pj_hi = sem("pj_hi")
        pj_read = sem("pj_read")
        back_made, back_read = sem("back_made"), sem("back_read")
        v_hi_done, v_split = sem("v_hi_done"), sem("v_split")
        scores, maxed, exped = sem("scores"), sem("maxed"), sem("exped")
        inverted, normed = sem("inverted"), sem("normed")
        transposed, pt_hi_done, pt_split = sem("transposed"), sem("pt_hi_done"), sem("pt_split")
        contexts, ct_hi_done, ct_split = sem("contexts"), sem("ct_hi_done"), sem("ct_split")
        bn, aggr, var_eps, rstd_done, ln_done = sem("bn"), sem("aggr"), sem("var_eps"), sem("rstd_done"), sem("ln_done")

        X, C, VS = 0, 2, 5
        HI_STEPS = VS
        ROUNDS = HEADS + 4
        PLAN = {0: [X], 1: [X + 1], 2: [C], 4: [C + 1], 7: [C + 2], 8: [VS], 9: [VS + 1]}
        W_DMAS = 3 * 16

        def step(half, u, k):
            return at(STEPS, half, u, k)

        def pj_bank(u, k):
            return pj_ps[(u + k) % 2]

        def head_rows(h):
            return slice((h % 2) * HEAD_DIM, (h % 2 + 1) * HEAD_DIM)

        def samples(half, u):
            return y[bass.ds(half * 2 + u, 1), :, :].rearrange("o (t p) d -> p (o t) d", p=P)

        block = ctx.enter_context(nc.Block())

        def layers(eng, begin, slot):
            with eng.Fori(0, LAYERS) as layer:
                first = layer * HALVES
                begin(layer, first)
                with eng.Fori(0, HALVES - 1) as pair:
                    half = first + pair
                    slot(half, 0, (half, 1))
                    slot(half, 1, (half + 1, 0))
                slot(first + (HALVES - 1), 0, (first + (HALVES - 1), 1))
                slot(first + (HALVES - 1), 1, None)

        @block.sync
        def _(sp):
            def load(half, pair, u):
                sp.dma_start(x_sb[u][:, :, :], samples(pair, u)).then_inc(x_loaded[u], 16)
                sp.dma_start(adj_sb[u][:, :, :], adj[bass.ds(pair * 2 + u, 1), :, :].rearrange("o (t p) d -> p (o t) d", p=P)).then_inc(x_loaded[u], 16)

            def load_weights(layer):
                sp.dma_start(w_stage[:, :, :, :], w[bass.ds(layer, 1), :, :].rearrange("o p n -> p (o n)").rearrange("p (m c n) -> p m c n", m=4, c=DC)).then_inc(w_loaded, 16)
                sp.dma_start(bc_stage[:, :, :], b_col[bass.ds(layer, 1), :, :].rearrange("o p n -> p (o n)").rearrange("p (m c) -> p m c", m=2)).then_inc(w_loaded, 16)
                sp.dma_start(br_stage[:, :, :], b_row[bass.ds(layer, 1), :].rearrange("o n -> (o n)").rearrange("(m n) -> m n", m=2).partition_broadcast(P)).then_inc(w_loaded, 16)

            def after_slot(half, pair, u, again):
                held(sp, back_read, CREDIT + at(NT, half, u, NT), passed)
                if again is not None:
                    load(half, again, u)
                held(sp, ln_done, at(NT, half, u, NT), passed)
                sp.dma_start(samples(pair, u), out_sb[u][:, :, :]).then_inc(stored[u], 16)

            def layer_samples(layer, more):
                first = layer * HALVES
                with sp.Fori(0, HALVES - 1) as pair:
                    for u in range(2):
                        after_slot(first + pair, pair, u, pair + 1)
                for u in range(2):
                    after_slot(first + (HALVES - 1), HALVES - 1, u, 0 if more else None)

            sp.dma_start(ident[:, :], ident_dram).then_inc(ident_loaded, 16)
            load(0, 0, 0)
            load_weights(0)
            load(0, 0, 1)
            with sp.Fori(0, LAYERS - 1) as layer:
                held(sp, w_split, layer * 4 + 4, passed)
                held(sp, b_ready, layer + 1, passed)
                load_weights(layer + 1)
                layer_samples(layer, True)
            layer_samples(LAYERS - 1, False)
            for u in range(2):
                sp.wait_ge(stored[u], 16 * HALVES * LAYERS)

        @block.gpsimd
        def _(pool):
            pool.memset(half_neg[:, :], -0.5).then_inc(half_ready, 1)
            for p in range(2):
                pool.memset(f32(v_hi[p][:, :, :, :]), 0.0).then_inc(zeros_ready, 1)
                pool.memset(f32(v_lo[p][:, :, :, :]), 0.0).then_inc(zeros_ready, 1)
            pool.wait_ge(half_ready, 1)
            pool.wait_ge(zeros_ready, 4)

            def make_mask(half, u):
                held(pool, x_loaded[u], half * 32 + 32, passed)
                pool.tensor_scalar(mask[u][:, :, :], adj_sb[u][:, :, :], -1.0, -NEG * HEAD_DIM ** 0.5, ALU.add, ALU.mult).then_inc(mask_ready, 1)

            def add_output_bias(half, u):
                pool.wait_ge(pj_made, step(half, u, C))
                for t in range(NT):
                    last = pool.tensor_tensor(x_sb[u][:, t, :], x_sb[u][:, t, :], br[:, 1, :], ALU.add)
                last.then_inc(x_biased, 1)

            def low_v(half, u, t):
                pool.wait_ge(v_hi_done, at(NT, half, u, t + 1))
                src = v[:, t, :].rearrange("p (h two d) -> p h two d", two=2, d=HEAD_DIM)
                for s in range(2):
                    hi, lo = (x[u][:, t, s::2, s * HEAD_DIM:(s + 1) * HEAD_DIM] for x in (v_hi, v_lo))
                    last = pool.tensor_tensor(lo, src[:, :, s, :], f32(hi), ALU.subtract)
                last.then_inc(v_split, 1)

            def normalise(half, u, h):
                held(pool, inverted, at(HEADS, half, u, h + 1), passed)
                i = (HEADS * u + h) % 4
                for t in range(NT):
                    last = pool.tensor_scalar(probs[:, i, t, :], probs[:, i, t, :], recs[:, u, h, t:t + 1], None, ALU.mult)
                last.then_inc(normed, 1)

            def inverse_std(half, u, t):
                held(pool, aggr, at(NT, half, u, t + 1), passed)
                pool.tensor_scalar(var[:, t:t + 1], mv[:, t, 1:2], EPS, None, ALU.add).then_inc(var_eps, 1)
                pool.wait_ge(var_eps, at(NT, half, u, t + 1))
                pool.tensor_tensor(rstd[:, t:t + 1], var[:, t:t + 1], half_neg[:, :], ALU.pow).then_inc(rstd_done, 1)

            def begin(layer, first):
                make_mask(first, 0)
                pool.wait_ge(b_ready, layer + 1)
                add_output_bias(first, 0)
                for t in range(NT):
                    low_v(first, 0, t)

            def slot(half, u, nxt):
                for j in range(ROUNDS):
                    if 0 <= j - 1 < HEADS:
                        normalise(half, u, j - 1)
                    if nxt and j == 1:
                        make_mask(*nxt)
                    if nxt and j == 3:
                        add_output_bias(*nxt)
                if nxt:
                    for t in range(NT):
                        low_v(*nxt, t)
                for t in range(NT):
                    inverse_std(half, u, t)

            layers(pool, begin, slot)

        @block.scalar
        def _(act):
            def hi_of_step(half, u, k):
                ps = pj_bank(u, k)
                if k >= VS:
                    t = k - VS
                    act.wait_ge(pj_read, step(half, u, k) + 1)
                    src = v[:, t, :].rearrange("p (h two d) -> p h two d", two=2, d=HEAD_DIM)
                    for s in range(2):
                        last = act.activation(v_hi[u][:, t, s::2, s * HEAD_DIM:(s + 1) * HEAD_DIM], src[:, :, s, :], ACT.Identity)
                    last.then_inc(v_hi_done, 1)
                    return
                act.wait_ge(pj_made, step(half, u, k) + 1)
                if k < C:
                    cols = slice((k - X) * P, (k - X + 1) * P)
                    act.activation(xt_hi[:, :, cols], ps[:, 0:D].rearrange("p (c n) -> p c n", c=DC), ACT.Identity).then_inc(pj_hi, 1)
                else:
                    c = k - C
                    for m in (Q, K):
                        last = act.activation(qk_hi[u][:, c, m, :], ps[:, m * N:(m + 1) * N], ACT.Identity, bias=bc[:, m, c:c + 1])
                    last.then_inc(pj_hi, 1)

            def begin(layer, first):
                act.wait_ge(w_loaded, layer * W_DMAS + W_DMAS)
                act.wait_ge(back_made, layer * (NT * B))
                for m in range(4):
                    act.activation(w_hi[:, m], w_stage[:, m], ACT.Identity).then_inc(w_hi_done, 1)
                act.wait_ge(b_ready, layer + 1)
                act.wait_ge(zeros_ready, 4)
                for k in range(STEPS):
                    hi_of_step(first, 0, k)

            def slot(half, u, nxt):
                for j in range(ROUNDS):
                    steps = PLAN.get(j, []) if nxt else []
                    for k in steps:
                        if k < VS:
                            hi_of_step(*nxt, k)
                    if 0 <= j - 3 < HEADS:
                        h = j - 3
                        act.wait_ge(transposed, at(HEADS, half, u, h + 1))
                        act.wait_ge(contexts, at(HEADS, half, u, max(h - 1, 0)))
                        act.activation(pt_hi[:, h % 2], pt_ps[h % 2][:, :, :], ACT.Identity).then_inc(pt_hi_done, 1)
                    if j < HEADS:
                        i = (HEADS * u + j) % 4
                        act.wait_ge(maxed, at(HEADS, half, u, j + 1))
                        act.wait_ge(transposed, at(HEADS, half, u, max(j - 3, 0)))
                        for t in range(NT):
                            last = act.activation(probs[:, i, t, :], logits[:, j % 2, t, :], ACT.Exp, scale=-1.0,
                                                  bias=nmax[:, u, j, t:t + 1], accum_out=sums[:, u, j, t:t + 1])
                        last.then_inc(exped, 1)
                    if 0 <= j - 4 < HEADS and (j - 4) % 2 == 1:
                        c = (j - 4) // 2
                        act.wait_ge(contexts, at(HEADS, half, u, 2 * c + 2))
                        act.wait_ge(back_made, at(NT, half, u, 0))
                        act.activation(ct_hi[:, c, :], cx_ps[(3 * u + c) % 2][:, 0:N], ACT.Identity).then_inc(ct_hi_done, 1)
                    for k in steps:
                        if k >= VS:
                            hi_of_step(*nxt, k)

            layers(act, begin, slot)

        @block.vector
        def _(dve):
            dve.sem_inc(back_read, CREDIT)

            def lo_of_step(half, u, k):
                ps = pj_bank(u, k)
                if k >= VS:
                    t = k - VS
                    dve.wait_ge(pj_made, step(half, u, k) + 1)
                    dve.wait_ge(v_split, at(NT, half, u, 0))
                    dve.tensor_tensor(v[:, t, :], ps[:, 0:D], br[:, 0, :], ALU.add).then_inc(pj_read, 1)
                    return
                dve.wait_ge(pj_hi, at(HI_STEPS, half, u, k + 1))
                if k < C:
                    cols = slice((k - X) * P, (k - X + 1) * P)
                    dve.tensor_tensor(xt_lo[:, :, cols], ps[:, 0:D].rearrange("p (c n) -> p c n", c=DC), f32(xt_hi[:, :, cols]), ALU.subtract).then_inc(pj_read, 1)
                else:
                    c = k - C
                    for m in (Q, K):
                        last = dve.scalar_tensor_tensor(qk_lo[u][:, c, m, :], ps[:, m * N:(m + 1) * N], bc[:, m, c:c + 1],
                                                        f32(qk_hi[u][:, c, m, :]), ALU.add, ALU.subtract)
                    last.then_inc(pj_read, 1)

            def invert(half, u, h):
                dve.wait_ge(exped, at(HEADS, half, u, h + 1))
                dve.reciprocal(recs[:, u, h, :], sums[:, u, h, :]).then_inc(inverted, 1)

            def begin(layer, first):
                dve.wait_ge(w_loaded, layer * W_DMAS + W_DMAS)
                dve.wait_ge(x_biased, layer * B)
                dve.wait_ge(pj_hi, layer * (HI_STEPS * B))
                dve.tensor_copy(bc[:, :, :], bc_stage[:, :, :])
                dve.tensor_copy(br[:, :, :], br_stage[:, :, :]).then_inc(b_ready, 1)
                dve.wait_ge(b_ready, layer + 1)
                for m in range(4):
                    dve.wait_ge(w_hi_done, layer * 4 + m + 1)
                    dve.tensor_tensor(w_lo[:, m], w_stage[:, m], f32(w_hi[:, m]), ALU.subtract).then_inc(w_split, 1)
                for k in range(STEPS):
                    lo_of_step(first, 0, k)

            def slot(half, u, nxt):
                for j in range(ROUNDS):
                    if 0 <= j - 1 < HEADS:
                        invert(half, u, j - 1)
                    if j < HEADS:
                        if j == 0:
                            dve.wait_ge(mask_ready, at(1, half, u, 1))
                        dve.wait_ge(scores, at(HEADS, half, u, j + 1))
                        held(dve, exped, at(HEADS, half, u, max(j - 1, 0)), passed)
                        for t in range(NT):
                            last = dve.tensor_tensor_reduce(
                                out=logits[:, j % 2, t, :], in0=s_ps[j % 2][:, t, :], in1=mask[u][:, t, :], scale=-HEAD_DIM ** -0.5,
                                scalar=BIG, op0=ALU.add, op1=ALU.min, accum_out=nmax[:, u, j, t:t + 1])
                        last.then_inc(maxed, 1)
                    if nxt:
                        for k in PLAN.get(j, []):
                            if k < VS:
                                lo_of_step(*nxt, k)
                    if 0 <= j - 3 < HEADS:
                        h = j - 3
                        dve.wait_ge(pt_hi_done, at(HEADS, half, u, h + 1))
                        dve.tensor_tensor(pt_lo[:, h % 2], pt_ps[h % 2][:, :, :], f32(pt_hi[:, h % 2]), ALU.subtract).then_inc(pt_split, 1)
                    if 0 <= j - 4 < HEADS and (j - 4) % 2 == 1:
                        c = (j - 4) // 2
                        dve.wait_ge(ct_hi_done, at(DC, half, u, c + 1))
                        dve.tensor_tensor(ct_lo[:, c, :], cx_ps[(3 * u + c) % 2][:, 0:N], f32(ct_hi[:, c, :]), ALU.subtract).then_inc(ct_split, 1)
                    if nxt:
                        for k in PLAN.get(j, []):
                            if k >= VS:
                                lo_of_step(*nxt, k)
                dve.wait_ge(x_biased, at(1, half, u, 1))
                for t in range(NT):
                    dve.wait_ge(back_made, at(NT, half, u, t + 1))
                    dve.tensor_tensor(mix[:, t, :], pj_bank(u, t)[:, 0:D], x_sb[u][:, t, :], ALU.add).then_inc(back_read, 1)
                    dve.wait_ge(back_read, CREDIT + at(NT, half, u, t + 1))
                    dve.bn_stats(stats[:, t, :], mix[:, t, :]).then_inc(bn, 1)
                    held(dve, bn, at(NT, half, u, t + 1), passed)
                    dve.bn_aggr(mv[:, t, :], stats[:, t, :]).then_inc(aggr, 1)
                dve.wait_ge(stored[u], half * 16)
                for t in range(NT):
                    dve.wait_ge(rstd_done, at(NT, half, u, t + 1))
                    dve.tensor_scalar(out_sb[u][:, t, :], mix[:, t, :], mv[:, t, 0:1], rstd[:, t:t + 1], ALU.subtract, ALU.mult).then_inc(ln_done, 1)

            layers(dve, begin, slot)

        @block.tensor
        def _(pe):
            def make_step(half, u, k, begins=False):
                ps = pj_bank(u, k)
                n = step(half, u, k)
                if k >= C:
                    pe.wait_ge(pj_read, n if k == C else n - 1)
                elif begins:
                    pe.wait_ge(back_read, CREDIT + at(NT, half, u, 0))
                else:
                    pe.wait_ge(pj_read, n - 1)
                    pe.wait_ge(back_read, CREDIT + at(NT, half, u, k - 3))
                if k < C:
                    t = k - X
                    pe.wait_ge(x_loaded[u], half * 32 + 32)
                    for c in range(DC):
                        last = pe.transpose(ps[:, c * P:(c + 1) * P], x_sb[u][:, t, c * P:(c + 1) * P], ident[:, :])
                elif k < VS:
                    cols = slice((k - C) * P, (k - C + 1) * P)
                    for m in (Q, K):
                        for c in range(DC):
                            last = product(pe, ps[:, m * N:(m + 1) * N], (w_hi[:, m, c, cols], w_lo[:, m, c, cols]), (xt_hi[:, c, :], xt_lo[:, c, :]),
                                           first=c == 0, last=c == DC - 1)
                else:
                    rows = slice((k - VS) * P, (k - VS + 1) * P)
                    for c in range(DC):
                        last = product(pe, ps[:, 0:D], (xt_hi[:, c, rows], xt_lo[:, c, rows]), (w_hi[:, V, c, :], w_lo[:, V, c, :]),
                                       first=c == 0, last=c == DC - 1)
                last.then_inc(pj_made, 1)

            def make_back(half, u, t, nxt):
                if t == 0:
                    pe.wait_ge(ct_split, at(DC, half, u, DC))
                if nxt:
                    pe.wait_ge(pj_read, step(*nxt, STEPS - 1 + t))
                else:
                    pe.wait_ge(back_read, CREDIT + at(NT, half, u, 0))
                rows = slice(t * P, (t + 1) * P)
                for c in range(DC):
                    last = product(pe, pj_bank(u, t)[:, 0:D], (ct_hi[:, c, rows], ct_lo[:, c, rows]), (w_hi[:, O, c, :], w_lo[:, O, c, :]),
                                   first=c == 0, last=c == DC - 1)
                last.then_inc(back_made, 1)

            def begin(layer, first):
                for k in range(STEPS):
                    if k == C:
                        pe.wait_ge(w_split, layer * 4 + 2)
                    if k == VS:
                        pe.wait_ge(w_split, layer * 4 + 4)
                    make_step(first, 0, k, begins=True)

            def slot(half, u, nxt):
                for j in range(ROUNDS):
                    if j < HEADS:
                        if j == 0:
                            pe.wait_ge(pj_read, step(half, u, VS))
                        pe.wait_ge(maxed, at(HEADS, half, u, max(j - 1, 0)))
                        c, rows = j // 2, head_rows(j)
                        for t in range(NT):
                            nodes = slice(t * P, (t + 1) * P)
                            last = product(pe, s_ps[j % 2][:, t, :], (qk_hi[u][rows, c, Q, nodes], qk_lo[u][rows, c, Q, nodes]),
                                           (qk_hi[u][rows, c, K, :], qk_lo[u][rows, c, K, :]))
                        last.then_inc(scores, 1)
                    steps = PLAN.get(j, []) if nxt else []
                    for k in steps:
                        if k < VS:
                            make_step(*nxt, k)
                    if 0 <= j - 3 < HEADS:
                        h = j - 3
                        i = (HEADS * u + h) % 4
                        pe.wait_ge(normed, at(HEADS, half, u, h + 1))
                        pe.wait_ge(pt_split, at(HEADS, half, u, max(h - 1, 0)))
                        for t in range(NT):
                            for kt in range(NT):
                                last = pe.transpose(pt_ps[h % 2][:, kt, t * P:(t + 1) * P], probs[:, i, t, kt * P:(kt + 1) * P], ident[:, :])
                        last.then_inc(transposed, 1)
                    if 0 <= j - 4 < HEADS:
                        h = j - 4
                        c = h // 2
                        pe.wait_ge(pt_split, at(HEADS, half, u, h + 1))
                        if h == 0:
                            pe.wait_ge(v_split, at(NT, half, u, NT))
                        if h % 2 == 0:
                            pe.wait_ge(ct_split, at(DC, half, u, max(c - 1, 0)))
                        for kt in range(NT):
                            last = product(pe, cx_ps[(3 * u + c) % 2][:, 0:N], (v_hi[u][:, kt, h, :], v_lo[u][:, kt, h, :]),
                                           (pt_hi[:, h % 2, kt, :], pt_lo[:, h % 2, kt, :]),
                                           first=h % 2 == 0 and kt == 0, last=h % 2 == 1 and kt == NT - 1)
                        last.then_inc(contexts, 1)
                    for k in steps:
                        if k >= VS:
                            make_step(*nxt, k)
                for t in range(NT):
                    make_back(half, u, t, nxt)

            pe.wait_ge(ident_loaded, 16)
            layers(pe, begin, slot)


def build(nc, x, adj, gat_w, gat_sd, gat_b, gat_hb, att_w, att_b_col, att_b_row, ident, sel, y):
    gat_phase(nc, x, adj, y, gat_w, gat_sd, gat_b, gat_hb, ident, sel)
    attention_phase(nc, y, adj, att_w, att_b_col, att_b_row, ident)


def kernel(**inputs):
    import numpy as np
    import concourse.bacc as bacc
    from concourse.bass_utils import run_bass_kernel_spmd

    a = {name: np.asarray(value) for name, value in inputs.items()}

    def rows_in(mats):
        return np.ascontiguousarray(np.stack([m.reshape(DC, P, -1) for m in mats]).transpose(2, 0, 1, 3))

    w_heads = a["L0_gnn_W"].transpose(1, 0, 2).reshape(D, D)
    w_sd = np.zeros((D, P), np.float32)
    for h in range(GAT_HEADS):
        rows = slice(h * GAT_DIM, (h + 1) * GAT_DIM)
        for q, name in enumerate(("L0_gnn_w_dst", "L0_gnn_w_dst", "L0_gnn_w_src", "L0_gnn_w_src")):
            w_sd[rows, 32 * q + h] = a[name][h, :, 0]
    sel = np.zeros((P, 2, GAT_HEADS), np.float32)
    for h in range(GAT_HEADS):
        for q in range(4):
            sel[32 * q + h, q // 2, h] = 1.0
    names = [f"L{layer}_gnn_" for layer in range(1, LAYERS + 1)]
    arrays = {
        "x": np.ascontiguousarray(a["x"]),
        "adj": np.ascontiguousarray(a["adj"]),
        "gat_w": rows_in([w_heads, a["L0_gnn_H_w"].T]),
        "gat_sd": rows_in([w_sd])[:, 0],
        "gat_b": np.ascontiguousarray(np.tile(a["L0_gnn_b"], P // GAT_DIM).reshape(P, 1)),
        "gat_hb": np.ascontiguousarray(a["L0_gnn_H_b"]),
        "att_w": np.stack([rows_in([a[n + m] for m in ("Wq", "Wk", "Wv", "Wf")]).reshape(P, -1) for n in names]),
        "att_b_col": np.stack([rows_in([a[n + m].reshape(D, 1) for m in ("bq", "bk")]).reshape(P, -1) for n in names]),
        "att_b_row": np.stack([np.concatenate([a[n + m] for m in ("bv", "bf")]) for n in names]),
        "ident": np.eye(P, dtype=np.float32),
        "sel": sel,
    }
    arrays = {n: np.ascontiguousarray(v) for n, v in arrays.items()}
    nc = bacc.Bacc("TRN2", target_bir_lowering=False, num_devices=1)
    drams = [nc.dram_tensor(n, v.shape, mybir.dt.from_np(v.dtype), kind="ExternalInput").ap() for n, v in arrays.items()]
    y = nc.dram_tensor("y", (B, N, D), F32, kind="ExternalOutput").ap()
    build(nc, *drams, y)
    return run_bass_kernel_spmd(nc, [arrays], core_ids=[0]).results[0]["y"]
```

```python
import concourse.bass as bass
from concourse import mybir
from contextlib import ExitStack

F32 = mybir.dt.float32
F32R = mybir.dt.float32r
BF16 = mybir.dt.bfloat16
U8 = mybir.dt.uint8
ALU = mybir.AluOpType
ACT = mybir.ActivationFunctionType

P = 128
B, N, D = 32, 256, 384
NT = N // P
DC = D // P
HALVES = B // 2
EPS = 1e-5

GAT_HEADS, GAT_DIM = 12, 32
HEADS, HEAD_DIM = 6, 64
LAYERS = 3

NEG = -9000000000000000.0
MASKED_GAT = -1e30
BIG = 3e38
START = 4


def at(per_unit, half, u, n):
    return half * (2 * per_unit) + (u * per_unit + n + START)


def start(eng, *sems):
    for s in sems:
        eng.sem_inc(s, START)


def f32(ap):
    return ap.bitcast(F32)


def every_slot(eng, first, slot):
    last = first + (HALVES - 1)
    slot(None, (first, 0), None)
    slot((first, 0), (first, 1), None)
    with eng.Fori(0, HALVES - 1) as pair:
        half = first + pair
        slot((half, 1), (half + 1, 0), (half, 0))
        slot((half + 1, 0), (half + 1, 1), (half, 1))
    slot((last, 1), None, (last, 0))
    slot(None, None, (last, 1))


def behind(cur, prev, heads, j, lag):
    unit, h = (cur, j - lag) if j >= lag else (prev, j - lag + heads)
    return (*unit, h) if unit else None


def held(eng, sem, value, passed):
    eng.wait_ge(sem, value)
    eng.sem_inc(passed, 1)


def product(pe, out, a, b, first=True, last=True):
    pe.matmul(out, a[1], b[0], start=first, stop=False)
    pe.matmul(out, a[0], b[1], start=False, stop=False)
    return pe.matmul(out, a[0], b[0], start=False, stop=last)


def gat_phase(nc, x, adj, y, w, w_sd, b_col, hb_row, ident_dram, sel_dram):
    STEPS = 9
    with ExitStack() as ctx:
        def sb(name, shape, dt=F32):
            return ctx.enter_context(nc.sbuf_tensor("g_" + name, shape, dt))

        def sem(name):
            return ctx.enter_context(nc.semaphore("g_" + name))

        x_sb = [sb(f"x{p}", [P, NT, D]) for p in range(2)]
        adj_sb = [sb(f"adj{p}", [P, NT, N], U8) for p in range(2)]
        mask = [sb(f"mask{p}", [P, NT, N], BF16) for p in range(2)]
        w_stage = sb("w_stage", [P, 2, DC, D])
        w_hi, w_lo = sb("w_hi", [P, 2, DC, D], F32R), sb("w_lo", [P, 2, DC, D], F32R)
        sd_stage = sb("sd_stage", [P, DC, P])
        sd_hi, sd_lo = sb("sd_hi", [P, DC, P], F32R), sb("sd_lo", [P, DC, P], F32R)
        b_sb = sb("b", [P, 1])
        hb_sb = sb("hb", [P, D])
        ident = sb("ident", [P, P])
        ident_bf = sb("ident_bf", [P, P], BF16)
        sel = sb("sel", [P, 2, GAT_HEADS])
        sel_dst = sb("sel_dst", [P, GAT_HEADS, P], F32R)
        sel_src = sb("sel_src", [P, GAT_HEADS, N], F32R)
        half_neg = sb("half_neg", [P, NT])
        xt_hi, xt_lo = sb("xt_hi", [P, DC, N], F32R), sb("xt_lo", [P, DC, N], F32R)
        th = sb("th", [P, NT, D])
        tt_hi, tt_lo = sb("tt_hi", [P, DC, N], F32R), sb("tt_lo", [P, DC, N], F32R)
        sd = [sb(f"sd{p}", [P, N], F32R) for p in range(2)]
        h_hi = [sb(f"h_hi{p}", [P, NT, GAT_HEADS, P], F32R) for p in range(2)]
        h_lo = [sb(f"h_lo{p}", [P, NT, GAT_HEADS, P], F32R) for p in range(2)]
        gate = [sb(f"gate{p}", [P, NT, D]) for p in range(2)]
        v_sb = sb("v", [P, 3, NT, N])
        probs = sb("probs", [P, 4, NT, N])
        nmax = sb("nmax", [P, 2, GAT_HEADS, NT])
        sums = sb("sums", [P, 2, GAT_HEADS, NT])
        recs = sb("recs", [P, 2, GAT_HEADS, NT])
        pt_hi, pt_lo = sb("pt_hi", [P, 2, NT, N], F32R), sb("pt_lo", [P, 2, NT, N], F32R)
        ct = sb("ct", [P, DC, N])
        ce = sb("ce", [P, DC, N])
        cx = sb("cx", [P, DC, N])
        residual = [sb(f"residual{p}", [P, NT, D]) for p in range(2)]
        mix = sb("mix", [P, NT, D])
        stats = sb("stats", [P, NT, 6])
        mv = sb("mv", [P, NT, 2])
        var = sb("var", [P, NT])
        rstd = sb("rstd", [P, NT])
        out_sb = [sb(f"out{p}", [P, NT, D]) for p in range(2)]
        z_ps = [ctx.enter_context(nc.psum_tensor(f"g_z{i}", [P, NT, N], F32)) for i in range(2)]
        pt_ps = [ctx.enter_context(nc.psum_tensor(f"g_pt{i}", [P, NT, N], F32)) for i in range(2)]
        cx_ps = [ctx.enter_context(nc.psum_tensor(f"g_cx{i}", [P, 512], F32)) for i in range(2)]
        pj_ps = [ctx.enter_context(nc.psum_tensor(f"g_pj{i}", [P, 512], F32)) for i in range(2)]

        passed = sem("passed")
        x_loaded = [sem(f"x_loaded{p}") for p in range(2)]
        stored = [sem(f"stored{p}") for p in range(2)]
        consts_loaded = sem("consts_loaded")
        consts_ready, zeros_ready, half_ready = sem("consts_ready"), sem("zeros_ready"), sem("half_ready")
        w_hi_done, w_split = sem("w_hi_done"), sem("w_split")
        mask_ready, x_kept = sem("mask_ready"), sem("x_kept")
        pj_made = sem("pj_made")
        pj_hi = sem("pj_hi")
        pj_read = sem("pj_read")
        back_made, back_read = sem("back_made"), sem("back_read")
        scores, lrelu, maxed = sem("scores"), sem("lrelu"), sem("maxed")
        exped, inverted, normed = sem("exped"), sem("inverted"), sem("normed")
        transposed, pt_hi_done, pt_split = sem("transposed"), sem("pt_hi_done"), sem("pt_split")
        contexts, ctx_read, ctx_min, ctx_exp, elu_done = (
            sem("contexts"), sem("ctx_read"), sem("ctx_min"), sem("ctx_exp"), sem("elu_done"))
        gate_done = sem("gate_done")
        gated, summed, bn, aggr = sem("gated"), sem("summed"), sem("bn"), sem("aggr")
        var_eps, rstd_done, ln_done = sem("var_eps"), sem("rstd_done"), sem("ln_done")

        X, H, TT, SD, G = 0, 2, 4, 6, 7
        BACK_AT = TT
        HI_STEPS = SD + 1
        PLAN = {0: X, 1: X + 1, 3: H, 4: H + 1, 7: TT, 8: TT + 1, 9: SD, 10: G, 11: G + 1}
        BACK_PLAN = {5: 0, 6: 1}
        T_LAG, C_LAG = 2, 3

        def step(half, u, k):
            return at(STEPS, half, u, k)

        def pj_bank(u, k):
            return pj_ps[(u + 1 + k) % 2]

        def back_bank(u, t):
            return pj_ps[(u + 1 + BACK_AT + t) % 2]

        block = ctx.enter_context(nc.Block())

        @block.sync
        def _(sp):
            def load(half, u):
                s = half * 2 + u
                sp.dma_start(x_sb[u][:, :, :], x[bass.ds(s, 1), :, :].rearrange("o (t p) d -> p (o t) d", p=P)).then_inc(x_loaded[u], 16)
                sp.dma_start(adj_sb[u][:, :, :], adj[bass.ds(s, 1), :, :].rearrange("o (t p) d -> p (o t) d", p=P)).then_inc(x_loaded[u], 16)

            def store(half, u):
                held(sp, ln_done, at(NT, half, u, NT), passed)
                sp.dma_start(y[bass.ds(half * 2 + u, 1), :, :].rearrange("o (t p) d -> p (o t) d", p=P), out_sb[u][:, :, :]).then_inc(stored[u], 16)

            start(sp, *stored)
            load(0, 0)
            for tile, source in ((ident, ident_dram), (sel, sel_dram), (w_stage, w), (sd_stage, w_sd), (b_sb, b_col)):
                sp.dma_start(tile[:], source).then_inc(consts_loaded, 16)
            sp.dma_start(hb_sb[:, :], hb_row.partition_broadcast(P)).then_inc(consts_loaded, 16)
            load(0, 1)

            def slot_of(nxt, prev, again):
                if again:
                    held(sp, x_kept, at(1, *nxt, 1), passed)
                    load(*again)
                if prev:
                    store(*prev)

            slot_of((0, 0), None, (1, 0))
            slot_of((0, 1), None, (1, 1))
            with sp.Fori(0, HALVES - 2) as half:
                slot_of((half + 1, 0), (half, 0), (half + 2, 0))
                slot_of((half + 1, 1), (half, 1), (half + 2, 1))
            for half in range(HALVES - 2, HALVES):
                for u in range(2):
                    store(half, u)
            for u in range(2):
                sp.wait_ge(stored[u], 16 * HALVES + START)

        @block.gpsimd
        def _(pool):
            start(pool, mask_ready, x_kept, normed, rstd_done, var_eps)
            pool.memset(half_neg[:, :], -0.5).then_inc(half_ready, 1)
            for p in range(2):
                pool.memset(f32(h_hi[p][:, :, :, :]), 0.0).then_inc(zeros_ready, 1)
                pool.memset(f32(h_lo[p][:, :, :, :]), 0.0).then_inc(zeros_ready, 1)

            def make_mask(half, u):
                held(pool, x_loaded[u], half * 32 + 32, passed)
                pool.tensor_scalar(mask[u][:, :, :], adj_sb[u][:, :, :], -1.0, -MASKED_GAT, ALU.add, ALU.mult).then_inc(mask_ready, 1)

            def inverse_std(half, u, eps):
                held(pool, aggr, at(NT, half, u, NT), passed)
                pool.tensor_scalar(var[:, :], mv[:, :, 1], eps, None, ALU.add).then_inc(var_eps, 1)
                pool.wait_ge(var_eps, at(1, half, u, 1))
                pool.tensor_tensor(rstd[:, :], var[:, :], half_neg[:, :], ALU.pow).then_inc(rstd_done, 1)

            def keep_x(half, u):
                pool.wait_ge(pj_made, step(half, u, H))
                held(pool, summed, at(NT, half, u, -NT), passed)
                pool.tensor_copy(residual[u][:, :, :], x_sb[u][:, :, :]).then_inc(x_kept, 1)

            def normalise(half, u, h):
                pool.wait_ge(inverted, at(GAT_HEADS, half, u, h + 1))
                i = h % 4
                pool.tensor_tensor(probs[:, i], probs[:, i], recs[:, u, h, :].unsqueeze(2).to_broadcast([P, NT, N]), ALU.mult).then_inc(normed, 1)

            def slot(cur, nxt, prev):
                for j in range(GAT_HEADS):
                    if head := behind(cur, prev, GAT_HEADS, j, 1):
                        normalise(*head)
                    if nxt and j == 2:
                        make_mask(*nxt)
                    if prev and j == 7:
                        inverse_std(*prev, 4 * EPS)
                    if nxt and j == 8:
                        keep_x(*nxt)

            pool.wait_ge(half_ready, 1)
            every_slot(pool, 0, slot)

        def padded(tile, t):
            g = tile[:, t, :, :].rearrange("p (c a) n -> p c (a n)", a=4)
            return [g[:, :, a * (P + GAT_DIM):a * (P + GAT_DIM) + GAT_DIM] for a in range(4)]

        @block.scalar
        def _(act):
            start(act, pj_hi, lrelu, exped, pt_hi_done, ctx_read, ctx_exp, gate_done)
            act.wait_ge(consts_loaded, 96)
            for m in range(2):
                act.activation(w_hi[:, m], w_stage[:, m], ACT.Identity).then_inc(w_hi_done, 1)
            act.activation(sd_hi[:, :, :], sd_stage[:, :, :], ACT.Identity).then_inc(w_hi_done, 1)
            act.wait_ge(zeros_ready, 4)

            def hi_of_step(half, u, k):
                ps = pj_bank(u, k)
                act.wait_ge(pj_made, step(half, u, k) + 1)
                if k in (X, X + 1):
                    t = k - X
                    act.activation(xt_hi[:, :, t * P:(t + 1) * P], ps[:, 0:D].rearrange("p (c n) -> p c n", c=DC), ACT.Identity).then_inc(pj_hi, 1)
                elif k in (H, H + 1):
                    t = k - H
                    act.activation(th[:, t, :], ps[:, 0:D], ACT.Tanh)
                    src = ps[:, 0:D].rearrange("p (c a e) -> p c a e", a=4, e=GAT_DIM)
                    for a, dst in enumerate(padded(h_hi[u], t)):
                        last = act.activation(dst, src[:, :, a, :], ACT.Identity)
                    last.then_inc(pj_hi, 1)
                elif k in (TT, TT + 1):
                    t = k - TT
                    act.activation(tt_hi[:, :, t * P:(t + 1) * P], ps[:, 0:D].rearrange("p (c n) -> p c n", c=DC), ACT.Identity).then_inc(pj_hi, 1)
                elif k == SD:
                    act.activation(sd[u][:, :], ps[:, 0:N], ACT.Identity).then_inc(pj_hi, 1)

            def gate_tanh(half, u, t):
                act.wait_ge(pj_read, step(half, u, G + t) + 1)
                act.activation(gate[u][:, t, :], gate[u][:, t, :], ACT.Tanh, scale=0.5).then_inc(gate_done, 1)

            def slot(cur, nxt, prev):
                for j in range(GAT_HEADS):
                    if cur:
                        act.wait_ge(scores, at(GAT_HEADS, *cur, j + 1))
                        act.wait_ge(exped, at(GAT_HEADS, *cur, j - 2))
                        act.activation(v_sb[:, j % 3], z_ps[j % 2][:, :, :], ACT.Relu, scale=-0.8).then_inc(lrelu, 1)
                    if head := behind(cur, prev, GAT_HEADS, j, T_LAG):
                        half, u, h = head
                        act.wait_ge(transposed, at(GAT_HEADS, half, u, h + 1))
                        act.wait_ge(contexts, at(GAT_HEADS, half, u, h - 1))
                        act.activation(pt_hi[:, h % 2], pt_ps[h % 2][:, :, :], ACT.Identity).then_inc(pt_hi_done, 1)
                    if cur:
                        half, u = cur
                        act.wait_ge(maxed, at(GAT_HEADS, half, u, j + 1))
                        act.wait_ge(transposed, at(GAT_HEADS, half, u, max(j - 3, -1)))
                        for t in range(NT):
                            last = act.activation(probs[:, j % 4, t, :], v_sb[:, j % 3, t, :], ACT.Exp, scale=-1.0,
                                                  bias=nmax[:, u, j, t:t + 1], accum_out=sums[:, u, j, t:t + 1])
                        last.then_inc(exped, 1)
                    head = behind(cur, prev, GAT_HEADS, j, C_LAG)
                    if head and head[2] % 4 == 3:
                        half, u, h = head
                        c = h // 4
                        act.wait_ge(contexts, at(GAT_HEADS, half, u, h + 1))
                        act.wait_ge(elu_done, at(1, half, u, 0))
                        act.activation(ct[:, c, :], cx_ps[(3 * u + c) % 2][:, 0:N], ACT.Identity, bias=b_sb[:, 0:1]).then_inc(ctx_read, 1)
                    if prev and j == 3:
                        act.wait_ge(ctx_min, at(1, *prev, 1))
                        act.activation(ce[:, :, :], ce[:, :, :], ACT.Exp).then_inc(ctx_exp, 1)
                    if nxt and j in PLAN and PLAN[j] < G:
                        hi_of_step(*nxt, PLAN[j])
                    if cur and j in (1, 2):
                        gate_tanh(*cur, j - 1)

            every_slot(act, 0, slot)

        @block.vector
        def _(dve):
            start(dve, pj_read, back_read, maxed, inverted, pt_split, ctx_min, elu_done, gated, summed, bn, aggr, ln_done)
            dve.wait_ge(consts_loaded, 96)
            dve.tensor_copy(ident_bf[:, :], ident[:, :])
            dve.tensor_copy(sel_dst[:, :, :], sel[:, 0, :].unsqueeze(2).to_broadcast([P, GAT_HEADS, P]))
            dve.tensor_copy(sel_src[:, :, :], sel[:, 1, :].unsqueeze(2).to_broadcast([P, GAT_HEADS, N])).then_inc(consts_ready, 1)
            for m in range(2):
                dve.wait_ge(w_hi_done, m + 1)
                dve.tensor_tensor(w_lo[:, m], w_stage[:, m], f32(w_hi[:, m]), ALU.subtract).then_inc(w_split, 1)
            dve.wait_ge(w_hi_done, 3)
            dve.tensor_tensor(sd_lo[:, :, :], sd_stage[:, :, :], f32(sd_hi[:, :, :]), ALU.subtract).then_inc(w_split, 1)

            def lo_of_step(half, u, k):
                ps = pj_bank(u, k)
                if k in (G, G + 1):
                    t = k - G
                    dve.wait_ge(pj_made, step(half, u, k) + 1)
                    dve.tensor_tensor(gate[u][:, t, :], ps[:, 0:D], hb_sb[:, :], ALU.add).then_inc(pj_read, 1)
                    return
                dve.wait_ge(pj_hi, at(HI_STEPS, half, u, k) + 1)
                if k in (X, X + 1):
                    cols = slice((k - X) * P, (k - X + 1) * P)
                    dve.tensor_tensor(xt_lo[:, :, cols], ps[:, 0:D].rearrange("p (c n) -> p c n", c=DC), f32(xt_hi[:, :, cols]), ALU.subtract).then_inc(pj_read, 1)
                elif k in (H, H + 1):
                    t = k - H
                    src = ps[:, 0:D].rearrange("p (c a e) -> p c a e", a=4, e=GAT_DIM)
                    for a, (hi, lo) in enumerate(zip(padded(h_hi[u], t), padded(h_lo[u], t))):
                        last = dve.tensor_tensor(lo, src[:, :, a, :], f32(hi), ALU.subtract)
                    last.then_inc(pj_read, 1)
                elif k in (TT, TT + 1):
                    cols = slice((k - TT) * P, (k - TT + 1) * P)
                    dve.tensor_tensor(tt_lo[:, :, cols], ps[:, 0:D].rearrange("p (c n) -> p c n", c=DC), f32(tt_hi[:, :, cols]), ALU.subtract).then_inc(pj_read, 1)
                elif k == SD:
                    for q in (1, 3):
                        rows = slice(32 * q, 32 * q + 32)
                        last = dve.tensor_tensor(sd[u][rows, :], ps[rows, 0:N], f32(sd[u][rows, :]), ALU.subtract)
                    last.then_inc(pj_read, 1)

            def invert(half, u, h):
                dve.wait_ge(exped, at(GAT_HEADS, half, u, h + 1))
                dve.reciprocal(recs[:, u, h, :], sums[:, u, h, :]).then_inc(inverted, 1)

            def mix_in(half, u, t):
                dve.wait_ge(x_kept, at(1, half, u, 1))
                dve.wait_ge(back_made, at(NT, half, u, t + 1))
                dve.tensor_tensor(mix[:, t, :], back_bank(u, t)[:, 0:D], residual[u][:, t, :], ALU.subtract).then_inc(back_read, 1)

            def gate_in(half, u):
                dve.wait_ge(gate_done, at(NT, half, u, NT))
                for t in range(NT):
                    dve.wait_ge(back_read, at(NT, half, u, t + 1))
                    dve.scalar_tensor_tensor(mix[:, t, :], gate[u][:, t, :], 1.0, mix[:, t, :], ALU.add, ALU.mult).then_inc(gated, 1)
                for t in range(NT):
                    dve.wait_ge(gated, at(NT, half, u, t + 1))
                    dve.scalar_tensor_tensor(mix[:, t, :], residual[u][:, t, :], 4.0, mix[:, t, :], ALU.mult, ALU.add).then_inc(summed, 1)
                for t in range(NT):
                    dve.wait_ge(summed, at(NT, half, u, t + 1))
                    dve.bn_stats(stats[:, t, :], mix[:, t, :]).then_inc(bn, 1)
                for t in range(NT):
                    held(dve, bn, at(NT, half, u, t + 1), passed)
                    dve.bn_aggr(mv[:, t, :], stats[:, t, :]).then_inc(aggr, 1)

            def layer_norm(half, u):
                dve.wait_ge(stored[u], half * 16 + START)
                dve.wait_ge(rstd_done, at(1, half, u, 1))
                for t in range(NT):
                    dve.tensor_scalar(out_sb[u][:, t, :], mix[:, t, :], mv[:, t, 0:1], rstd[:, t:t + 1], ALU.subtract, ALU.mult).then_inc(ln_done, 1)

            def slot(cur, nxt, prev):
                for j in range(GAT_HEADS):
                    if cur:
                        held(dve, lrelu, at(GAT_HEADS, *cur, j + 1), passed)
                        for t in range(NT):
                            last = dve.tensor_tensor_reduce(
                                out=v_sb[:, j % 3, t, :], in0=z_ps[j % 2][:, t, :], in1=v_sb[:, j % 3, t, :], scale=-1.0,
                                scalar=BIG, op0=ALU.add, op1=ALU.min, accum_out=nmax[:, cur[1], j, t:t + 1])
                        last.then_inc(maxed, 1)
                    if head := behind(cur, prev, GAT_HEADS, j, 1):
                        invert(*head)
                    if head := behind(cur, prev, GAT_HEADS, j, T_LAG):
                        half, u, h = head
                        dve.wait_ge(pt_hi_done, at(GAT_HEADS, half, u, h + 1))
                        dve.tensor_tensor(pt_lo[:, h % 2], pt_ps[h % 2][:, :, :], f32(pt_hi[:, h % 2]), ALU.subtract).then_inc(pt_split, 1)
                    if prev and j == 2:
                        dve.wait_ge(ctx_read, at(DC, *prev, DC))
                        dve.tensor_scalar(ce[:, :, :], ct[:, :, :], 0.0, None, ALU.min).then_inc(ctx_min, 1)
                    if nxt and j in PLAN:
                        lo_of_step(*nxt, PLAN[j])
                    if prev and j == 3:
                        dve.wait_ge(ctx_exp, at(1, *prev, 1))
                        dve.scalar_tensor_tensor(cx[:, :, :], ce[:, :, :], -1.0, ct[:, :, :], ALU.add, ALU.max).then_inc(elu_done, 1)
                    if prev and j in BACK_PLAN:
                        mix_in(*prev, BACK_PLAN[j])
                    if prev and j == 6:
                        gate_in(*prev)
                    if prev and j == 7:
                        layer_norm(*prev)

            every_slot(dve, 0, slot)

        @block.tensor
        def _(pe):
            start(pe, pj_made, back_made, scores, transposed, contexts)

            def make_step(half, u, k):
                ps = pj_bank(u, k)
                n = step(half, u, k)
                pe.wait_ge(pj_read, n if k in (H, SD) else n - 1)
                if k in (BACK_AT, BACK_AT + 1):
                    pe.wait_ge(back_read, at(NT, half, u, k - BACK_AT - 3))
                if k in (X, X + 1):
                    t = k - X
                    pe.wait_ge(x_loaded[u], half * 32 + 32)
                    for c in range(DC):
                        last = pe.transpose(ps[:, c * P:(c + 1) * P], x_sb[u][:, t, c * P:(c + 1) * P], ident[:, :])
                elif k in (H, H + 1, G, G + 1):
                    m = 0 if k in (H, H + 1) else 1
                    t = k - (H, G)[m]
                    rows = slice(t * P, (t + 1) * P)
                    for c in range(DC):
                        last = product(pe, ps[:, 0:D], (xt_hi[:, c, rows], xt_lo[:, c, rows]), (w_hi[:, m, c, :], w_lo[:, m, c, :]),
                                       first=c == 0, last=c == DC - 1)
                elif k in (TT, TT + 1):
                    t = k - TT
                    for c in range(DC):
                        last = pe.transpose(ps[:, c * P:(c + 1) * P], th[:, t, c * P:(c + 1) * P], ident[:, :])
                else:
                    for c in range(DC):
                        last = product(pe, ps[:, 0:N], (sd_hi[:, c, :], sd_lo[:, c, :]), (tt_hi[:, c, :], tt_lo[:, c, :]),
                                       first=c == 0, last=c == DC - 1)
                last.then_inc(pj_made, 1)

            def make_back(half, u, t, nxt):
                if t == 0:
                    pe.wait_ge(elu_done, at(1, half, u, 1))
                if nxt:
                    pe.wait_ge(pj_read, step(*nxt, BACK_AT - 1 + t))
                else:
                    pe.wait_ge(pj_read, step(half, u, STEPS))
                    pe.wait_ge(back_read, at(NT, half, u, 0))
                for c in range(DC):
                    last = pe.transpose(back_bank(u, t)[:, c * P:(c + 1) * P], cx[:, c, t * P:(t + 1) * P], ident[:, :])
                last.then_inc(back_made, 1)

            def slot(cur, nxt, prev):
                for j in range(GAT_HEADS):
                    if cur:
                        half, u = cur
                        if j == 0:
                            pe.wait_ge(pj_read, step(half, u, SD) + 1)
                            pe.wait_ge(mask_ready, at(1, half, u, 1))
                        pe.wait_ge(maxed, at(GAT_HEADS, half, u, j - 1))
                        for t in range(NT):
                            z = z_ps[j % 2][:, t, :]
                            pe.matmul(z, sel_dst[:, j, :], sd[u][:, :], start=True, stop=False)
                            pe.matmul(z, sd[u][:, t * P:(t + 1) * P], sel_src[:, j, :], start=False, stop=False)
                            last = pe.matmul(z, ident_bf[:, :], mask[u][:, t, :], start=False, stop=True)
                        last.then_inc(scores, 1)
                    if nxt and j in PLAN:
                        make_step(*nxt, PLAN[j])
                    if prev and j in BACK_PLAN:
                        make_back(*prev, BACK_PLAN[j], nxt)
                    if head := behind(cur, prev, GAT_HEADS, j, T_LAG):
                        half, u, h = head
                        pe.wait_ge(normed, at(GAT_HEADS, half, u, h + 1))
                        pe.wait_ge(pt_split, at(GAT_HEADS, half, u, h - 1))
                        for t in range(NT):
                            for kt in range(NT):
                                last = pe.transpose(pt_ps[h % 2][:, kt, t * P:(t + 1) * P], probs[:, h % 4, t, kt * P:(kt + 1) * P], ident[:, :])
                        last.then_inc(transposed, 1)
                    if head := behind(cur, prev, GAT_HEADS, j, C_LAG):
                        half, u, h = head
                        c = h // 4
                        pe.wait_ge(pt_split, at(GAT_HEADS, half, u, h + 1))
                        if h % 4 == 0:
                            pe.wait_ge(ctx_read, at(DC, half, u, c - 1))
                        for kt in range(NT):
                            last = product(pe, cx_ps[(3 * u + c) % 2][:, 0:N], (h_hi[u][:, kt, h, :], h_lo[u][:, kt, h, :]),
                                           (pt_hi[:, h % 2, kt, :], pt_lo[:, h % 2, kt, :]),
                                           first=h % 4 == 0 and kt == 0, last=h % 4 == 3 and kt == NT - 1)
                        last.then_inc(contexts, 1)

            pe.wait_ge(consts_loaded, 96)
            pe.wait_ge(consts_ready, 1)
            pe.wait_ge(w_split, 3)
            every_slot(pe, 0, slot)


def attention_phase(nc, y, adj, w, b_col, b_row, ident_dram):
    STEPS = 7
    Q, K, V, O = range(4)
    with ExitStack() as ctx:
        def sb(name, shape, dt=F32):
            return ctx.enter_context(nc.sbuf_tensor("a_" + name, shape, dt))

        def sem(name):
            return ctx.enter_context(nc.semaphore("a_" + name))

        x_sb = [sb(f"x{p}", [P, NT, D]) for p in range(2)]
        adj_sb = [sb(f"adj{p}", [P, NT, N], U8) for p in range(2)]
        mask = [sb(f"mask{p}", [P, NT, N]) for p in range(2)]
        w_stage = sb("w_stage", [P, 4, DC, D])
        w_hi, w_lo = sb("w_hi", [P, 4, DC, D], F32R), sb("w_lo", [P, 4, DC, D], F32R)
        bc_stage, br_stage = sb("bc_stage", [P, 2, DC]), sb("br_stage", [P, 2, D])
        bc, br = sb("bc", [P, 2, DC]), sb("br", [P, 2, D])
        ident = sb("ident", [P, P])
        half_neg = sb("half_neg", [P, NT])
        xt_hi, xt_lo = sb("xt_hi", [P, DC, N], F32R), sb("xt_lo", [P, DC, N], F32R)
        qk_hi = [sb(f"qk_hi{p}", [P, DC, 2, N], F32R) for p in range(2)]
        qk_lo = [sb(f"qk_lo{p}", [P, DC, 2, N], F32R) for p in range(2)]
        v = sb("v", [P, NT, D])
        v_hi = [sb(f"v_hi{p}", [P, NT, HEADS, P], F32R) for p in range(2)]
        v_lo = [sb(f"v_lo{p}", [P, NT, HEADS, P], F32R) for p in range(2)]
        logits = sb("logits", [P, 2, NT, N])
        probs = sb("probs", [P, 4, NT, N])
        nmax = sb("nmax", [P, 2, HEADS, NT])
        sums = sb("sums", [P, 2, HEADS, NT])
        recs = sb("recs", [P, 2, HEADS, NT])
        pt_hi, pt_lo = sb("pt_hi", [P, 2, NT, N], F32R), sb("pt_lo", [P, 2, NT, N], F32R)
        ct_hi, ct_lo = sb("ct_hi", [P, DC, N], F32R), sb("ct_lo", [P, DC, N], F32R)
        residual = [sb(f"residual{p}", [P, NT, D]) for p in range(2)]
        mix = sb("mix", [P, NT, D])
        stats = sb("stats", [P, NT, 6])
        mv = sb("mv", [P, NT, 2])
        var = sb("var", [P, NT])
        rstd = sb("rstd", [P, NT])
        out_sb = [sb(f"out{p}", [P, NT, D]) for p in range(2)]
        s_ps = [ctx.enter_context(nc.psum_tensor(f"a_s{i}", [P, NT, N], F32)) for i in range(2)]
        pt_ps = [ctx.enter_context(nc.psum_tensor(f"a_pt{i}", [P, NT, N], F32)) for i in range(2)]
        cx_ps = [ctx.enter_context(nc.psum_tensor(f"a_cx{i}", [P, 512], F32)) for i in range(2)]
        pj_ps = [ctx.enter_context(nc.psum_tensor(f"a_pj{i}", [P, 512], F32)) for i in range(2)]

        passed = sem("passed")
        x_loaded = [sem(f"x_loaded{p}") for p in range(2)]
        stored = [sem(f"stored{p}") for p in range(2)]
        ident_loaded, w_loaded = sem("ident_loaded"), sem("w_loaded")
        half_ready, zeros_ready = sem("half_ready"), sem("zeros_ready")
        w_hi_done, w_split, b_ready = sem("w_hi_done"), sem("w_split"), sem("b_ready")
        mask_ready, x_biased = sem("mask_ready"), sem("x_biased")
        pj_made = sem("pj_made")
        pj_hi = sem("pj_hi")
        pj_read = sem("pj_read")
        back_made, back_read = sem("back_made"), sem("back_read")
        v_hi_done, v_split = sem("v_hi_done"), sem("v_split")
        scores, maxed, exped = sem("scores"), sem("maxed"), sem("exped")
        inverted, normed = sem("inverted"), sem("normed")
        transposed, pt_hi_done, pt_split = sem("transposed"), sem("pt_hi_done"), sem("pt_split")
        contexts, ct_hi_done, ct_split = sem("contexts"), sem("ct_hi_done"), sem("ct_split")
        bn, aggr, var_eps, rstd_done, ln_done = sem("bn"), sem("aggr"), sem("var_eps"), sem("rstd_done"), sem("ln_done")

        X, C, VS = 0, 2, 5
        HI_STEPS = VS
        BACK_AT = VS
        PLAN = {0: X, 2: C + 1, 3: C + 2, 5: VS + 1}
        LATE_PLAN = {0: X + 1, 1: C, 4: VS}
        BACK_PLAN, LATE_BACK_PLAN = {4: 1}, {3: 0}
        T_LAG, C_LAG = 2, 3
        W_DMAS = 3 * 16

        def step(half, u, k):
            return at(STEPS, half, u, k)

        def pj_bank(u, k):
            return pj_ps[(u + 1 + k) % 2]

        def back_bank(u, t):
            return pj_ps[(u + 1 + BACK_AT + t) % 2]

        def head_rows(h):
            return slice((h % 2) * HEAD_DIM, (h % 2 + 1) * HEAD_DIM)

        def samples(half, u):
            return y[bass.ds(half * 2 + u, 1), :, :].rearrange("o (t p) d -> p (o t) d", p=P)

        block = ctx.enter_context(nc.Block())

        def layers(eng, begin, slot):
            with eng.Fori(0, LAYERS) as layer:
                begin(layer)
                every_slot(eng, layer * HALVES, slot)

        @block.sync
        def _(sp):
            def load(pair, u):
                sp.dma_start(x_sb[u][:, :, :], samples(pair, u)).then_inc(x_loaded[u], 16)
                sp.dma_start(adj_sb[u][:, :, :], adj[bass.ds(pair * 2 + u, 1), :, :].rearrange("o (t p) d -> p (o t) d", p=P)).then_inc(x_loaded[u], 16)

            def load_weights(layer):
                sp.dma_start(w_stage[:, :, :, :], w[bass.ds(layer, 1), :, :].rearrange("o p n -> p (o n)").rearrange("p (m c n) -> p m c n", m=4, c=DC)).then_inc(w_loaded, 16)
                sp.dma_start(bc_stage[:, :, :], b_col[bass.ds(layer, 1), :, :].rearrange("o p n -> p (o n)").rearrange("p (m c) -> p m c", m=2)).then_inc(w_loaded, 16)
                sp.dma_start(br_stage[:, :, :], b_row[bass.ds(layer, 1), :].rearrange("o n -> (o n)").rearrange("(m n) -> m n", m=2).partition_broadcast(P)).then_inc(w_loaded, 16)

            def store(half, pair, u):
                held(sp, ln_done, at(NT, half, u, NT), passed)
                sp.dma_start(samples(pair, u), out_sb[u][:, :, :]).then_inc(stored[u], 16)

            def load_again(half, u, pair):
                held(sp, x_biased, at(1, half, u, 1), passed)
                load(pair, u)

            def layer_samples(layer, more):
                first = layer * HALVES
                for u in range(2):
                    load_again(first, u, 1)
                with sp.Fori(0, HALVES - 2) as pair:
                    for u in range(2):
                        load_again(first + pair + 1, u, pair + 2)
                        store(first + pair, pair, u)
                for u in range(2):
                    if more:
                        load_again(first + (HALVES - 1), u, 0)
                    store(first + (HALVES - 2), HALVES - 2, u)
                for u in range(2):
                    store(first + (HALVES - 1), HALVES - 1, u)

            start(sp, *stored)
            sp.dma_start(ident[:, :], ident_dram).then_inc(ident_loaded, 16)
            load(0, 0)
            load_weights(0)
            load(0, 1)
            with sp.Fori(0, LAYERS - 1) as layer:
                held(sp, w_split, layer * 4 + 4, passed)
                held(sp, b_ready, layer + 1, passed)
                load_weights(layer + 1)
                layer_samples(layer, True)
            layer_samples(LAYERS - 1, False)
            for u in range(2):
                sp.wait_ge(stored[u], 16 * HALVES * LAYERS + START)

        @block.gpsimd
        def _(pool):
            start(pool, mask_ready, x_biased, v_split, rstd_done, var_eps)
            pool.memset(half_neg[:, :], -0.5).then_inc(half_ready, 1)
            for p in range(2):
                pool.memset(f32(v_hi[p][:, :, :, :]), 0.0).then_inc(zeros_ready, 1)
                pool.memset(f32(v_lo[p][:, :, :, :]), 0.0).then_inc(zeros_ready, 1)
            pool.wait_ge(half_ready, 1)
            pool.wait_ge(zeros_ready, 4)

            def make_mask(half, u):
                held(pool, x_loaded[u], half * 32 + 32, passed)
                pool.tensor_scalar(mask[u][:, :, :], adj_sb[u][:, :, :], -1.0, -NEG * HEAD_DIM ** 0.5, ALU.add, ALU.mult).then_inc(mask_ready, 1)

            def add_output_bias(half, u):
                pool.wait_ge(pj_made, step(half, u, C))
                pool.wait_ge(back_read, at(NT, half, u, -NT))
                for t in range(NT):
                    last = pool.tensor_tensor(residual[u][:, t, :], x_sb[u][:, t, :], br[:, 1, :], ALU.add)
                last.then_inc(x_biased, 1)

            def low_v(half, u, t):
                pool.wait_ge(v_hi_done, at(NT, half, u, t + 1))
                src = v[:, t, :].rearrange("p (h two d) -> p h two d", two=2, d=HEAD_DIM)
                for s in range(2):
                    hi, lo = (x[u][:, t, s::2, s * HEAD_DIM:(s + 1) * HEAD_DIM] for x in (v_hi, v_lo))
                    last = pool.tensor_tensor(lo, src[:, :, s, :], f32(hi), ALU.subtract)
                last.then_inc(v_split, 1)

            def inverse_std(half, u, eps):
                held(pool, aggr, at(NT, half, u, NT), passed)
                pool.tensor_scalar(var[:, :], mv[:, :, 1], eps, None, ALU.add).then_inc(var_eps, 1)
                pool.wait_ge(var_eps, at(1, half, u, 1))
                pool.tensor_tensor(rstd[:, :], var[:, :], half_neg[:, :], ALU.pow).then_inc(rstd_done, 1)

            def begin(layer):
                pool.wait_ge(b_ready, layer + 1)

            def slot(cur, nxt, prev):
                for j in range(HEADS):
                    if nxt and j == 0:
                        make_mask(*nxt)
                    if nxt and j == 5:
                        add_output_bias(*nxt)
                        for t in range(NT):
                            low_v(*nxt, t)
                    if prev and j == 4:
                        inverse_std(*prev, EPS)

            layers(pool, begin, slot)

        @block.scalar
        def _(act):
            start(act, pj_hi, v_hi_done, exped, pt_hi_done, ct_hi_done)
            def hi_of_step(half, u, k):
                ps = pj_bank(u, k)
                if k >= VS:
                    t = k - VS
                    act.wait_ge(pj_read, step(half, u, k) + 1)
                    src = v[:, t, :].rearrange("p (h two d) -> p h two d", two=2, d=HEAD_DIM)
                    for s in range(2):
                        last = act.activation(v_hi[u][:, t, s::2, s * HEAD_DIM:(s + 1) * HEAD_DIM], src[:, :, s, :], ACT.Identity)
                    last.then_inc(v_hi_done, 1)
                    return
                act.wait_ge(pj_made, step(half, u, k) + 1)
                if k < C:
                    cols = slice((k - X) * P, (k - X + 1) * P)
                    act.activation(xt_hi[:, :, cols], ps[:, 0:D].rearrange("p (c n) -> p c n", c=DC), ACT.Identity).then_inc(pj_hi, 1)
                else:
                    c = k - C
                    for m in (Q, K):
                        last = act.activation(qk_hi[u][:, c, m, :], ps[:, m * N:(m + 1) * N], ACT.Identity, bias=bc[:, m, c:c + 1])
                    last.then_inc(pj_hi, 1)

            def begin(layer):
                act.wait_ge(w_loaded, layer * W_DMAS + W_DMAS)
                act.wait_ge(back_made, layer * (NT * B) + START)
                for m in range(4):
                    act.activation(w_hi[:, m], w_stage[:, m], ACT.Identity).then_inc(w_hi_done, 1)
                act.wait_ge(b_ready, layer + 1)
                act.wait_ge(zeros_ready, 4)

            def slot(cur, nxt, prev):
                for j in range(HEADS):
                    if nxt and j - 1 in LATE_PLAN:
                        hi_of_step(*nxt, LATE_PLAN[j - 1])
                    if cur:
                        half, u = cur
                        i = (HEADS * u + j) % 4
                        act.wait_ge(maxed, at(HEADS, half, u, j + 1))
                        act.wait_ge(transposed, at(HEADS, half, u, max(j - 3, -1)))
                        for t in range(NT):
                            last = act.activation(probs[:, i, t, :], logits[:, j % 2, t, :], ACT.Exp, scale=-1.0,
                                                  bias=nmax[:, u, j, t:t + 1], accum_out=sums[:, u, j, t:t + 1])
                        last.then_inc(exped, 1)
                    if nxt and j in PLAN:
                        hi_of_step(*nxt, PLAN[j])
                    if head := behind(cur, prev, HEADS, j, T_LAG):
                        half, u, h = head
                        act.wait_ge(transposed, at(HEADS, half, u, h + 1))
                        act.wait_ge(contexts, at(HEADS, half, u, h - 1))
                        act.activation(pt_hi[:, h % 2], pt_ps[h % 2][:, :, :], ACT.Identity).then_inc(pt_hi_done, 1)
                    head = behind(cur, prev, HEADS, j, C_LAG)
                    if head and head[2] % 2 == 1:
                        half, u, h = head
                        c = h // 2
                        act.wait_ge(contexts, at(HEADS, half, u, h + 1))
                        act.wait_ge(back_made, at(NT, half, u, 0))
                        act.activation(ct_hi[:, c, :], cx_ps[(3 * u + c) % 2][:, 0:N], ACT.Identity).then_inc(ct_hi_done, 1)

            layers(act, begin, slot)

        @block.vector
        def _(dve):
            start(dve, pj_read, back_read, maxed, inverted, normed, pt_split, ct_split, bn, aggr, ln_done)

            def lo_of_step(half, u, k):
                ps = pj_bank(u, k)
                if k >= VS:
                    t = k - VS
                    dve.wait_ge(pj_made, step(half, u, k) + 1)
                    dve.wait_ge(v_split, at(NT, half, u, 0))
                    dve.tensor_tensor(v[:, t, :], ps[:, 0:D], br[:, 0, :], ALU.add).then_inc(pj_read, 1)
                    return
                dve.wait_ge(pj_hi, at(HI_STEPS, half, u, k + 1))
                if k < C:
                    cols = slice((k - X) * P, (k - X + 1) * P)
                    dve.tensor_tensor(xt_lo[:, :, cols], ps[:, 0:D].rearrange("p (c n) -> p c n", c=DC), f32(xt_hi[:, :, cols]), ALU.subtract).then_inc(pj_read, 1)
                else:
                    c = k - C
                    for m in (Q, K):
                        last = dve.scalar_tensor_tensor(qk_lo[u][:, c, m, :], ps[:, m * N:(m + 1) * N], bc[:, m, c:c + 1],
                                                        f32(qk_hi[u][:, c, m, :]), ALU.add, ALU.subtract)
                    last.then_inc(pj_read, 1)

            def normalise(half, u, h):
                dve.wait_ge(exped, at(HEADS, half, u, h + 1))
                dve.reciprocal(recs[:, u, h, :], sums[:, u, h, :]).then_inc(inverted, 1)
                dve.wait_ge(inverted, at(HEADS, half, u, h + 1))
                for t in range(NT):
                    last = dve.tensor_scalar(probs[:, (HEADS * u + h) % 4, t, :], probs[:, (HEADS * u + h) % 4, t, :], recs[:, u, h, t:t + 1], None, ALU.mult)
                last.then_inc(normed, 1)

            def begin(layer):
                dve.wait_ge(w_loaded, layer * W_DMAS + W_DMAS)
                dve.wait_ge(x_biased, layer * B + START)
                dve.wait_ge(pj_hi, layer * (HI_STEPS * B) + START)
                dve.tensor_copy(bc[:, :, :], bc_stage[:, :, :])
                dve.tensor_copy(br[:, :, :], br_stage[:, :, :]).then_inc(b_ready, 1)
                dve.wait_ge(b_ready, layer + 1)
                for m in range(4):
                    dve.wait_ge(w_hi_done, layer * 4 + m + 1)
                    dve.tensor_tensor(w_lo[:, m], w_stage[:, m], f32(w_hi[:, m]), ALU.subtract).then_inc(w_split, 1)

            def add_back(half, u, t):
                dve.wait_ge(x_biased, at(1, half, u, 1))
                dve.wait_ge(back_made, at(NT, half, u, t + 1))
                dve.tensor_tensor(mix[:, t, :], back_bank(u, t)[:, 0:D], residual[u][:, t, :], ALU.add).then_inc(back_read, 1)

            def statistics(half, u):
                for t in range(NT):
                    dve.wait_ge(back_read, at(NT, half, u, t + 1))
                    dve.bn_stats(stats[:, t, :], mix[:, t, :]).then_inc(bn, 1)
                for t in range(NT):
                    held(dve, bn, at(NT, half, u, t + 1), passed)
                    dve.bn_aggr(mv[:, t, :], stats[:, t, :]).then_inc(aggr, 1)

            def layer_norm(half, u):
                dve.wait_ge(stored[u], half * 16 + START)
                dve.wait_ge(rstd_done, at(1, half, u, 1))
                for t in range(NT):
                    dve.tensor_scalar(out_sb[u][:, t, :], mix[:, t, :], mv[:, t, 0:1], rstd[:, t:t + 1], ALU.subtract, ALU.mult).then_inc(ln_done, 1)

            def slot(cur, nxt, prev):
                for j in range(HEADS):
                    if cur:
                        half, u = cur
                        if j == 0:
                            dve.wait_ge(mask_ready, at(1, half, u, 1))
                        dve.wait_ge(scores, at(HEADS, half, u, j + 1))
                        held(dve, exped, at(HEADS, half, u, j - 1), passed)
                        for t in range(NT):
                            last = dve.tensor_tensor_reduce(
                                out=logits[:, j % 2, t, :], in0=s_ps[j % 2][:, t, :], in1=mask[u][:, t, :], scale=-HEAD_DIM ** -0.5,
                                scalar=BIG, op0=ALU.add, op1=ALU.min, accum_out=nmax[:, u, j, t:t + 1])
                        last.then_inc(maxed, 1)
                    if nxt and j - 1 in LATE_PLAN:
                        lo_of_step(*nxt, LATE_PLAN[j - 1])
                    if prev and j - 1 in LATE_BACK_PLAN:
                        add_back(*prev, LATE_BACK_PLAN[j - 1])
                    if head := behind(cur, prev, HEADS, j, 1):
                        normalise(*head)
                    if nxt and j in PLAN:
                        lo_of_step(*nxt, PLAN[j])
                    if prev and j in BACK_PLAN:
                        add_back(*prev, BACK_PLAN[j])
                    if head := behind(cur, prev, HEADS, j, T_LAG):
                        half, u, h = head
                        dve.wait_ge(pt_hi_done, at(HEADS, half, u, h + 1))
                        dve.tensor_tensor(pt_lo[:, h % 2], pt_ps[h % 2][:, :, :], f32(pt_hi[:, h % 2]), ALU.subtract).then_inc(pt_split, 1)
                    head = behind(cur, prev, HEADS, j, C_LAG)
                    if head and head[2] % 2 == 1:
                        half, u, h = head
                        c = h // 2
                        dve.wait_ge(ct_hi_done, at(DC, half, u, c + 1))
                        dve.tensor_tensor(ct_lo[:, c, :], cx_ps[(3 * u + c) % 2][:, 0:N], f32(ct_hi[:, c, :]), ALU.subtract).then_inc(ct_split, 1)
                    if prev and j == 4:
                        statistics(*prev)
                    if prev and j == 5:
                        layer_norm(*prev)

            layers(dve, begin, slot)

        @block.tensor
        def _(pe):
            def make_step(half, u, k):
                ps = pj_bank(u, k)
                n = step(half, u, k)
                pe.wait_ge(pj_read, n if k == C else n - 1)
                if k in (BACK_AT, BACK_AT + 1):
                    pe.wait_ge(back_read, at(NT, half, u, k - BACK_AT - 3))
                if k < C:
                    t = k - X
                    pe.wait_ge(x_loaded[u], half * 32 + 32)
                    for c in range(DC):
                        last = pe.transpose(ps[:, c * P:(c + 1) * P], x_sb[u][:, t, c * P:(c + 1) * P], ident[:, :])
                elif k < VS:
                    cols = slice((k - C) * P, (k - C + 1) * P)
                    for m in (Q, K):
                        for c in range(DC):
                            last = product(pe, ps[:, m * N:(m + 1) * N], (w_hi[:, m, c, cols], w_lo[:, m, c, cols]), (xt_hi[:, c, :], xt_lo[:, c, :]),
                                           first=c == 0, last=c == DC - 1)
                else:
                    rows = slice((k - VS) * P, (k - VS + 1) * P)
                    for c in range(DC):
                        last = product(pe, ps[:, 0:D], (xt_hi[:, c, rows], xt_lo[:, c, rows]), (w_hi[:, V, c, :], w_lo[:, V, c, :]),
                                       first=c == 0, last=c == DC - 1)
                last.then_inc(pj_made, 1)

            def make_back(half, u, t, nxt):
                if t == 0:
                    pe.wait_ge(ct_split, at(DC, half, u, DC))
                if nxt:
                    pe.wait_ge(pj_read, step(*nxt, BACK_AT - 1 + t))
                else:
                    pe.wait_ge(pj_read, step(half, u, STEPS))
                    pe.wait_ge(back_read, at(NT, half, u, 0))
                rows = slice(t * P, (t + 1) * P)
                for c in range(DC):
                    last = product(pe, back_bank(u, t)[:, 0:D], (ct_hi[:, c, rows], ct_lo[:, c, rows]), (w_hi[:, O, c, :], w_lo[:, O, c, :]),
                                   first=c == 0, last=c == DC - 1)
                last.then_inc(back_made, 1)

            def begin(layer):
                pe.wait_ge(w_split, layer * 4 + 4)
                pe.wait_ge(back_read, layer * (NT * B) + START)

            def slot(cur, nxt, prev):
                for j in range(HEADS):
                    if cur:
                        half, u = cur
                        if j == 0:
                            pe.wait_ge(pj_read, step(half, u, VS))
                        pe.wait_ge(maxed, at(HEADS, half, u, j - 1))
                        c, rows = j // 2, head_rows(j)
                        for t in range(NT):
                            nodes = slice(t * P, (t + 1) * P)
                            last = product(pe, s_ps[j % 2][:, t, :], (qk_hi[u][rows, c, Q, nodes], qk_lo[u][rows, c, Q, nodes]),
                                           (qk_hi[u][rows, c, K, :], qk_lo[u][rows, c, K, :]))
                        last.then_inc(scores, 1)
                    if nxt and j in PLAN:
                        make_step(*nxt, PLAN[j])
                    if prev and j in BACK_PLAN:
                        make_back(*prev, BACK_PLAN[j], nxt)
                    if head := behind(cur, prev, HEADS, j, T_LAG):
                        half, u, h = head
                        i = (HEADS * u + h) % 4
                        pe.wait_ge(normed, at(HEADS, half, u, h + 1))
                        pe.wait_ge(pt_split, at(HEADS, half, u, h - 1))
                        for t in range(NT):
                            for kt in range(NT):
                                last = pe.transpose(pt_ps[h % 2][:, kt, t * P:(t + 1) * P], probs[:, i, t, kt * P:(kt + 1) * P], ident[:, :])
                        last.then_inc(transposed, 1)
                    if head := behind(cur, prev, HEADS, j, C_LAG):
                        half, u, h = head
                        c = h // 2
                        pe.wait_ge(pt_split, at(HEADS, half, u, h + 1))
                        if h == 0:
                            pe.wait_ge(v_split, at(NT, half, u, NT))
                        if h % 2 == 0:
                            pe.wait_ge(ct_split, at(DC, half, u, c - 1))
                        for kt in range(NT):
                            last = product(pe, cx_ps[(3 * u + c) % 2][:, 0:N], (v_hi[u][:, kt, h, :], v_lo[u][:, kt, h, :]),
                                           (pt_hi[:, h % 2, kt, :], pt_lo[:, h % 2, kt, :]),
                                           first=h % 2 == 0 and kt == 0, last=h % 2 == 1 and kt == NT - 1)
                        last.then_inc(contexts, 1)
                    if nxt and j in LATE_PLAN:
                        make_step(*nxt, LATE_PLAN[j])
                    if prev and j in LATE_BACK_PLAN:
                        make_back(*prev, LATE_BACK_PLAN[j], nxt)

            start(pe, pj_made, back_made, scores, transposed, contexts)
            pe.wait_ge(ident_loaded, 16)
            layers(pe, begin, slot)


def build(nc, x, adj, gat_w, gat_sd, gat_b, gat_hb, att_w, att_b_col, att_b_row, ident, sel, y):
    gat_phase(nc, x, adj, y, gat_w, gat_sd, gat_b, gat_hb, ident, sel)
    attention_phase(nc, y, adj, att_w, att_b_col, att_b_row, ident)


def kernel(**inputs):
    import numpy as np
    import concourse.bacc as bacc
    from concourse.bass_utils import run_bass_kernel_spmd

    a = {name: np.asarray(value) for name, value in inputs.items()}

    def rows_in(mats):
        return np.ascontiguousarray(np.stack([m.reshape(DC, P, -1) for m in mats]).transpose(2, 0, 1, 3))

    w_heads = a["L0_gnn_W"].transpose(1, 0, 2).reshape(D, D)
    w_sd = np.zeros((D, P), np.float32)
    for h in range(GAT_HEADS):
        rows = slice(h * GAT_DIM, (h + 1) * GAT_DIM)
        for q, name in enumerate(("L0_gnn_w_dst", "L0_gnn_w_dst", "L0_gnn_w_src", "L0_gnn_w_src")):
            w_sd[rows, 32 * q + h] = a[name][h, :, 0]
    sel = np.zeros((P, 2, GAT_HEADS), np.float32)
    for h in range(GAT_HEADS):
        for q in range(4):
            sel[32 * q + h, q // 2, h] = 1.0
    names = [f"L{layer}_gnn_" for layer in range(1, LAYERS + 1)]
    arrays = {
        "x": np.ascontiguousarray(a["x"]),
        "adj": np.ascontiguousarray(a["adj"]),
        "gat_w": rows_in([w_heads, a["L0_gnn_H_w"].T]),
        "gat_sd": rows_in([w_sd])[:, 0],
        "gat_b": np.ascontiguousarray(np.tile(a["L0_gnn_b"], P // GAT_DIM).reshape(P, 1)),
        "gat_hb": np.ascontiguousarray(a["L0_gnn_H_b"]),
        "att_w": np.stack([rows_in([a[n + m] for m in ("Wq", "Wk", "Wv", "Wf")]).reshape(P, -1) for n in names]),
        "att_b_col": np.stack([rows_in([a[n + m].reshape(D, 1) for m in ("bq", "bk")]).reshape(P, -1) for n in names]),
        "att_b_row": np.stack([np.concatenate([a[n + m] for m in ("bv", "bf")]) for n in names]),
        "ident": np.eye(P, dtype=np.float32),
        "sel": sel,
    }
    arrays = {n: np.ascontiguousarray(v) for n, v in arrays.items()}
    nc = bacc.Bacc("TRN2", target_bir_lowering=False, num_devices=1)
    drams = [nc.dram_tensor(n, v.shape, mybir.dt.from_np(v.dtype), kind="ExternalInput").ap() for n, v in arrays.items()]
    y = nc.dram_tensor("y", (B, N, D), F32, kind="ExternalOutput").ap()
    build(nc, *drams, y)
    return run_bass_kernel_spmd(nc, [arrays], core_ids=[0]).results[0]["y"]
```

```python
import concourse.bass as bass
from concourse import mybir
from contextlib import ExitStack

F32 = mybir.dt.float32
F32R = mybir.dt.float32r
BF16 = mybir.dt.bfloat16
U8 = mybir.dt.uint8
ALU = mybir.AluOpType
ACT = mybir.ActivationFunctionType

P = 128
B, N, D = 32, 256, 384
NT = N // P
DC = D // P
HALVES = B // 2
UNROLLED = 5
EPS = 1e-5

GAT_HEADS, GAT_DIM = 12, 32
HEADS, HEAD_DIM = 6, 64
LAYERS = 3

NEG = -9000000000000000.0
MASKED_GAT = -1e30
BIG = 3e38
START = 4


def at(per_unit, half, u, n):
    return half * (2 * per_unit) + (u * per_unit + n + START)


def start(eng, *sems):
    for s in sems:
        eng.sem_inc(s, START)


def f32(ap):
    return ap.bitcast(F32)


def every_slot(eng, first, slot):
    last = first + (HALVES - 1)
    slot(None, (first, 0), None)
    slot((first, 0), (first, 1), None)
    with eng.Fori(0, (HALVES - 1) // UNROLLED) as i:
        for pair in range(UNROLLED):
            half = first + i * UNROLLED + pair
            slot((half, 1), (half + 1, 0), (half, 0))
            slot((half + 1, 0), (half + 1, 1), (half, 1))
    slot((last, 1), None, (last, 0))
    slot(None, None, (last, 1))


def behind(cur, prev, heads, j, lag):
    unit, h = (cur, j - lag) if j >= lag else (prev, j - lag + heads)
    return (*unit, h) if unit else None


def held(eng, sem, value, passed):
    eng.wait_ge(sem, value)
    eng.sem_inc(passed, 1)


def product(pe, out, a, b, first=True, last=True):
    pe.matmul(out, a[1], b[0], start=first, stop=False)
    pe.matmul(out, a[0], b[1], start=False, stop=False)
    return pe.matmul(out, a[0], b[0], start=False, stop=last)


def gat_phase(nc, x, adj, y, w, w_sd, b_row, hb_rows, ident_dram, sel_dram, fold_dram, att_w, att_w_stage, att_w_loaded):
    STEPS = 9
    GROUPS = GAT_HEADS // 2
    with ExitStack() as ctx:
        def sb(name, shape, dt=F32):
            return ctx.enter_context(nc.sbuf_tensor("g_" + name, shape, dt))

        def sem(name):
            return ctx.enter_context(nc.semaphore("g_" + name))

        x_sb = [sb(f"x{p}", [P, NT, D]) for p in range(2)]
        adj_sb = [sb(f"adj{p}", [P, NT, N], U8) for p in range(2)]
        mask = [sb(f"mask{p}", [P, NT, N], BF16) for p in range(2)]
        w_stage = sb("w_stage", [P, 2, DC, D])
        w_hi, w_lo = sb("w_hi", [P, 2, DC, D], F32R), sb("w_lo", [P, 2, DC, D], F32R)
        sd_stage = sb("sd_stage", [P, DC, P])
        sd_hi, sd_lo = sb("sd_hi", [P, DC, P], F32R), sb("sd_lo", [P, DC, P], F32R)
        b_sb = sb("b", [P, D])
        hb_stage, hb_hi, hb = sb("hb_stage", [2 * 32, D]), sb("hb_hi", [2 * 32, D], F32R), sb("hb", [2 * 32, D], F32R)
        ones = sb("ones", [2 * 32, P], F32R)
        ident = sb("ident", [P, P])
        ident_bf = sb("ident_bf", [P, P], BF16)
        sel = sb("sel", [P, 2, GAT_HEADS])
        fold = sb("fold", [P, 2 * GAT_DIM])
        sel_dst = sb("sel_dst", [P, GAT_HEADS, P], F32R)
        sel_src = sb("sel_src", [P, GAT_HEADS, N], F32R)
        half_neg = sb("half_neg", [P, NT])
        xt_hi, xt_lo = sb("xt_hi", [P, DC, N], F32R), sb("xt_lo", [P, DC, N], F32R)
        th = sb("th", [P, NT, D])
        tt_hi, tt_lo = sb("tt_hi", [P, DC, N], F32R), sb("tt_lo", [P, DC, N], F32R)
        sd = [sb(f"sd{p}", [P, N], F32R) for p in range(2)]
        h_split = [sb(f"h_split{p}", [P, NT, GAT_HEADS, P], F32R) for p in range(2)]
        gate = [sb(f"gate{p}", [P, NT, D]) for p in range(2)]
        v_sb = sb("v", [P, 3, NT, N])
        exps = sb("exps", [P, 4, NT, N])
        nmax = sb("nmax", [P, 2, GAT_HEADS, NT])
        sums = sb("sums", [P, 2, GAT_HEADS, NT])
        recs = sb("recs", [P, 2, GAT_HEADS, NT])
        pt_hi, pt_lo = sb("pt_hi", [P, 3, NT, N], F32R), sb("pt_lo", [P, 3, NT, N], F32R)
        ct = [sb(f"ct{p}", [P, GROUPS, N]) for p in range(2)]
        cx = sb("cx", [P, NT, D])
        ce = sb("ce", [P, NT, D])
        residual = [sb(f"residual{p}", [P, NT, D]) for p in range(2)]
        mix = sb("mix", [P, NT, D])
        stats = sb("stats", [P, NT, 6])
        mv = sb("mv", [P, NT, 2])
        var = sb("var", [P, NT])
        rstd = sb("rstd", [P, NT])
        out_sb = [sb(f"out{p}", [P, NT, D]) for p in range(2)]
        z_ps = [ctx.enter_context(nc.psum_tensor(f"g_z{i}", [P, NT, N], F32)) for i in range(2)]
        pt_ps = [ctx.enter_context(nc.psum_tensor(f"g_pt{i}", [P, NT, N], F32)) for i in range(2)]
        cx_ps = [ctx.enter_context(nc.psum_tensor(f"g_cx{i}", [P, 512], F32)) for i in range(2)]
        pj_ps = [ctx.enter_context(nc.psum_tensor(f"g_pj{i}", [P, 512], F32)) for i in range(2)]

        passed = sem("passed")
        x_loaded = [sem(f"x_loaded{p}") for p in range(2)]
        stored = [sem(f"stored{p}") for p in range(2)]
        consts_loaded = sem("consts_loaded")
        consts_ready, zeros_ready, half_ready = sem("consts_ready"), sem("zeros_ready"), sem("half_ready")
        w_hi_done, w_split, hb_ready = sem("w_hi_done"), sem("w_split"), sem("hb_ready")
        mask_ready, x_share, x_used = sem("mask_ready"), sem("x_share"), sem("x_used")
        pj_made = sem("pj_made")
        pj_hi = sem("pj_hi")
        hi_copied = sem("hi_copied")
        pj_read = sem("pj_read")
        back_made, back_read = sem("back_made"), sem("back_read")
        scores, lrelu, maxed = sem("scores"), sem("lrelu"), sem("maxed")
        exped, inverted = sem("exped"), sem("inverted")
        transposed, pt_hi_done, pt_split = sem("transposed"), sem("pt_hi_done"), sem("pt_split")
        contexts, ctx_read, ctx_bias, ctx_min, ctx_exp, elu_done = (
            sem("contexts"), sem("ctx_read"), sem("ctx_bias"), sem("ctx_min"), sem("ctx_exp"), sem("elu_done"))
        gate_done = sem("gate_done")
        gated, summed, bn, aggr = sem("gated"), sem("summed"), sem("bn"), sem("aggr")
        var_eps, rstd_done, ln_done = sem("var_eps"), sem("rstd_done"), sem("ln_done")

        X, H, TT, G, SD, LAST = 0, 2, 4, 6, 7, 8
        ALL = tuple(range(DC))
        PE_PLAN = {0: [(X, ALL)], 1: [], 2: [(X + 1, ALL)], 3: [(H, (0, 1))], 4: [(H, (2,))], 5: [(H + 1, (0, 1))], 6: [(H + 1, (2,))],
                   7: [(TT, ALL)], 8: [(TT + 1, ALL)], 9: [(G, ALL)], 10: [(SD, ALL)], 11: [(LAST, ALL)]}
        PLAN = {j: k for j, made in PE_PLAN.items() for k, chunks in made if DC - 1 in chunks}
        BACK_PLAN = {4: 0, 5: 1}
        BANK = {X: 0, X + 1: 1, H: 0, H + 1: 0, TT: 1, TT + 1: 0, G: 1, SD: 0, LAST: 1}
        HI_STEPS = {H: 1, H + 1: 2, SD: 3}
        READ_STEPS = {X: 1, X + 1: 2, H: 3, H + 1: 4, TT: 5, TT + 1: 6, SD: 7}
        COPY_STEPS = {X: 1, X + 1: 2, TT: 3, TT + 1: 4}
        T_LAG, C_LAG = 2, 4

        def step(half, u, k):
            return at(STEPS, half, u, k)

        def reads(half, u, k):
            return at(len(READ_STEPS), half, u, READ_STEPS[k])

        def pj_bank(k):
            return pj_ps[BANK[k]]

        back_bank = pj_ps[1]

        block = ctx.enter_context(nc.Block())

        @block.sync
        def _(sp):
            def load(half, u):
                s = half * 2 + u
                sp.dma_start(x_sb[u][:, :, :], x[bass.ds(s, 1), :, :].rearrange("o (t p) d -> p (o t) d", p=P)).then_inc(x_loaded[u], 16)
                sp.dma_start(adj_sb[u][:, :, :], adj[bass.ds(s, 1), :, :].rearrange("o (t p) d -> p (o t) d", p=P)).then_inc(x_loaded[u], 16)

            def store(half, u):
                held(sp, ln_done, at(NT, half, u, NT), passed)
                sp.dma_start(y[bass.ds(half * 2 + u, 1), :, :].rearrange("o (t p) d -> p (o t) d", p=P), out_sb[u][:, :, :]).then_inc(stored[u], 16)

            start(sp, *stored)
            load(0, 0)
            for tile, source in ((ident, ident_dram), (sel, sel_dram), (fold, fold_dram), (w_stage, w), (sd_stage, w_sd), (hb_stage, hb_rows)):
                sp.dma_start(tile[:], source).then_inc(consts_loaded, 16)
            sp.dma_start(b_sb[:, :], b_row.partition_broadcast(P)).then_inc(consts_loaded, 16)
            load(0, 1)
            load_att_weights(sp, att_w, 0, att_w_stage, att_w_loaded)

            def load_again(half, u):
                held(sp, x_used, at(1, half, u, 1), passed)
                load(half + 1, u)

            load_again(0, 0)
            load_again(0, 1)
            store(0, 0)
            with sp.Fori(0, HALVES - 2) as i:
                load_again(i + 1, 0)
                store(i, 1)
                load_again(i + 1, 1)
                store(i + 1, 0)
            store(HALVES - 2, 1)
            store(HALVES - 1, 0)
            store(HALVES - 1, 1)
            for u in range(2):
                sp.wait_ge(stored[u], 16 * HALVES + START)

        @block.gpsimd
        def _(pool):
            start(pool, mask_ready, x_share, x_used, ctx_bias, summed, rstd_done, var_eps, ln_done)
            pool.memset(half_neg[:, :], -0.5).then_inc(half_ready, 1)
            for p in range(2):
                pool.memset(f32(h_split[p][:, :, :, :]), 0.0).then_inc(zeros_ready, 1)

            def make_mask(half, u, prev):
                if prev:
                    pool.wait_ge(scores, at(GAT_HEADS, *prev, GAT_HEADS))
                held(pool, x_loaded[u], half * 32 + 32, passed)
                pool.tensor_scalar(mask[u][:, :, :], adj_sb[u][:, :, :], -1.0, -MASKED_GAT, ALU.add, ALU.mult).then_inc(mask_ready, 1)

            def inverse_std(half, u, eps):
                held(pool, aggr, at(NT, half, u, NT), passed)
                pool.tensor_scalar(var[:, :], mv[:, :, 1], eps, None, ALU.add).then_inc(var_eps, 1)
                pool.wait_ge(var_eps, at(1, half, u, 1))
                pool.tensor_tensor(rstd[:, :], var[:, :], half_neg[:, :], ALU.pow).then_inc(rstd_done, 1)

            def add_bias(half, u):
                for t in range(NT):
                    pool.wait_ge(back_read, at(NT, half, u, t + 1))
                    last = pool.tensor_tensor(cx[:, t, :], cx[:, t, :], b_sb[:, :], ALU.add)
                last.then_inc(ctx_bias, 1)

            def total(half, u):
                held(pool, gated, at(1, half, u, 1), passed)
                pool.tensor_tensor(mix[:, :, :], mix[:, :, :], residual[u][:, :, :], ALU.add).then_inc(summed, 1)

            def share_of_x(half, u):
                pool.wait_ge(summed, at(1, half, u, -1))
                held(pool, gate_done, at(NT, half, u, NT), passed)
                pool.tensor_scalar(residual[u][:, :, :], gate[u][:, :, :], -1.0, 3.0, ALU.mult, ALU.add).then_inc(x_share, 1)
                pool.wait_ge(x_share, at(1, half, u, 1))
                pool.tensor_tensor(residual[u][:, :, :], residual[u][:, :, :], x_sb[u][:, :, :], ALU.mult).then_inc(x_used, 1)

            def layer_norm(half, u):
                pool.wait_ge(stored[u], half * 16 + START)
                held(pool, rstd_done, at(1, half, u, 1), passed)
                for t in range(NT):
                    pool.tensor_scalar(out_sb[u][:, t, :], mix[:, t, :], mv[:, t, 0:1], rstd[:, t:t + 1], ALU.subtract, ALU.mult).then_inc(ln_done, 1)

            def slot(cur, nxt, prev):
                for j in range(GAT_HEADS):
                    if nxt and j == 2:
                        make_mask(*nxt, prev)
                    if cur and j == 4:
                        share_of_x(*cur)
                    if prev and j == 6:
                        add_bias(*prev)
                    if prev and j == 9:
                        total(*prev)
                    if prev and j == 11:
                        inverse_std(*prev, 4 * EPS)
                        layer_norm(*prev)

            pool.wait_ge(half_ready, 1)
            every_slot(pool, 0, slot)

        def parts(u, t):
            g = h_split[u][:, t, :, :].rearrange("p (c b) n -> p c (b n)", b=2)
            firsts = (0, P + 2 * GAT_DIM)
            return [(g[:, :, f:f + GAT_DIM], g[:, :, f + GAT_DIM:f + 2 * GAT_DIM]) for f in firsts]

        @block.scalar
        def _(act):
            start(act, pj_hi, lrelu, exped, pt_hi_done, ctx_read, ctx_exp, gate_done)
            act.wait_ge(consts_loaded, 7 * 16)
            for m in range(2):
                act.activation(w_hi[:, m], w_stage[:, m], ACT.Identity).then_inc(w_hi_done, 1)
            act.activation(sd_hi[:, :, :], sd_stage[:, :, :], ACT.Identity).then_inc(w_hi_done, 1)
            act.activation(hb_hi[:, :], hb_stage[:, :], ACT.Identity).then_inc(w_hi_done, 1)
            act.wait_ge(w_hi_done, 4)
            act.activation(hb[0:32, :], hb_hi[0:32, :], ACT.Identity)
            act.activation(ones[:, :], hb_stage[:, 0:P], ACT.Identity, scale=0.0, bias=1.0).then_inc(hb_ready, 1)
            act.wait_ge(zeros_ready, 2)

            def hi_of_step(half, u, k, prev):
                ps = pj_bank(k)
                act.wait_ge(pj_made, step(half, u, k) + 1)
                if k == SD:
                    act.activation(sd[u][:, :], ps[:, 0:N], ACT.Identity).then_inc(pj_hi, 1)
                    return
                t = k - H
                act.activation(th[:, t, :], ps[:, 0:D], ACT.Tanh)
                src = ps[:, 0:D].rearrange("p (c b e) -> p c b e", b=2, e=GAT_DIM)
                if prev:
                    act.wait_ge(contexts, at(GAT_HEADS, *prev, GAT_HEADS))
                for b, (hi, _) in enumerate(parts(u, t)):
                    last = act.activation(hi, src[:, :, b, :], ACT.Identity)
                last.then_inc(pj_hi, 1)

            def gate_tanh(half, u, k):
                t = 0 if k == G else 1
                act.wait_ge(x_used, at(1, half, u, -1))
                act.wait_ge(gated, at(1, half, u, -1))
                act.wait_ge(pj_made, step(half, u, k) + 1)
                act.activation(gate[u][:, t, :], pj_bank(k)[:, 0:D], ACT.Tanh, scale=0.5).then_inc(gate_done, 1)

            def slot(cur, nxt, prev):
                for j in range(GAT_HEADS):
                    if cur:
                        act.wait_ge(scores, at(GAT_HEADS, *cur, j + 1))
                        act.wait_ge(exped, at(GAT_HEADS, *cur, j - 2))
                        act.activation(v_sb[:, j % 3], z_ps[j % 2][:, :, :], ACT.Relu, scale=-0.8).then_inc(lrelu, 1)
                    if head := behind(cur, prev, GAT_HEADS, j, 1):
                        half, u, h = head
                        act.wait_ge(maxed, at(GAT_HEADS, half, u, h + 1))
                        act.wait_ge(transposed, at(GAT_HEADS, half, u, h - 3))
                        for t in range(NT):
                            last = act.activation(exps[:, h % 4, t, :], v_sb[:, h % 3, t, :], ACT.Exp, scale=-1.0,
                                                  bias=nmax[:, u, h, t:t + 1], accum_out=sums[:, u, h, t:t + 1])
                        last.then_inc(exped, 1)
                    if nxt and PLAN.get(j) in HI_STEPS:
                        hi_of_step(*nxt, PLAN[j], prev)
                    if head := behind(cur, prev, GAT_HEADS, j, T_LAG):
                        half, u, h = head
                        act.wait_ge(transposed, at(GAT_HEADS, half, u, h + 1))
                        act.wait_ge(contexts, at(GAT_HEADS, half, u, h - 2))
                        act.activation(pt_hi[:, h % 3], pt_ps[h % 2][:, :, :], ACT.Identity).then_inc(pt_hi_done, 1)
                    head = behind(cur, prev, GAT_HEADS, j, C_LAG)
                    if head and head[2] % 2 == 1:
                        half, u, h = head
                        c = h // 2
                        act.wait_ge(contexts, at(GAT_HEADS, half, u, h + 1))
                        act.activation(ct[u][:, c, :], cx_ps[c % 2][:, 0:N], ACT.Identity).then_inc(ctx_read, 1)
                    if prev and j == 8:
                        act.wait_ge(ctx_min, at(1, *prev, 1))
                        act.activation(ce[:, :, :], ce[:, :, :], ACT.Exp).then_inc(ctx_exp, 1)
                    if nxt and PLAN.get(j) in (G, LAST):
                        gate_tanh(*nxt, PLAN[j])

            every_slot(act, 0, slot)

        @block.vector
        def _(dve):
            start(dve, pj_read, hi_copied, back_read, maxed, inverted, pt_split, ctx_min, elu_done, gated, bn, aggr)
            dve.wait_ge(consts_loaded, 7 * 16)
            dve.tensor_copy(ident_bf[:, :], ident[:, :])
            dve.tensor_copy(sel_dst[:, :, :], sel[:, 0, :].unsqueeze(2).to_broadcast([P, GAT_HEADS, P]))
            dve.tensor_copy(sel_src[:, :, :], sel[:, 1, :].unsqueeze(2).to_broadcast([P, GAT_HEADS, N])).then_inc(consts_ready, 1)
            for m in range(2):
                dve.wait_ge(w_hi_done, m + 1)
                dve.tensor_tensor(w_lo[:, m], w_stage[:, m], f32(w_hi[:, m]), ALU.subtract).then_inc(w_split, 1)
            dve.wait_ge(w_hi_done, 3)
            dve.tensor_tensor(sd_lo[:, :, :], sd_stage[:, :, :], f32(sd_hi[:, :, :]), ALU.subtract).then_inc(w_split, 1)
            dve.wait_ge(w_hi_done, 4)
            dve.tensor_tensor(hb[32:64, :], hb_stage[32:64, :], f32(hb_hi[32:64, :]), ALU.subtract).then_inc(w_split, 1)

            def lo_of_step(half, u, k):
                ps = pj_bank(k)
                if k in COPY_STEPS:
                    hi, lo, first = (xt_hi, xt_lo, X) if k < H else (tt_hi, tt_lo, TT)
                    cols = slice((k - first) * P, (k - first + 1) * P)
                    src = ps[:, 0:D].rearrange("p (c n) -> p c n", c=DC)
                    dve.wait_ge(pj_made, step(half, u, k) + 1)
                    dve.tensor_copy(hi[:, :, cols], src).then_inc(hi_copied, 1)
                    dve.wait_ge(hi_copied, at(len(COPY_STEPS), half, u, COPY_STEPS[k]))
                    dve.tensor_tensor(lo[:, :, cols], src, f32(hi[:, :, cols]), ALU.subtract).then_inc(pj_read, 1)
                    return
                dve.wait_ge(pj_hi, at(len(HI_STEPS), half, u, HI_STEPS[k]))
                if k in (H, H + 1):
                    src = ps[:, 0:D].rearrange("p (c b e) -> p c b e", b=2, e=GAT_DIM)
                    for b, (hi, lo) in enumerate(parts(u, k - H)):
                        last = dve.tensor_tensor(lo, src[:, :, b, :], f32(hi), ALU.subtract)
                    last.then_inc(pj_read, 1)
                elif k == SD:
                    for q in (1, 3):
                        rows = slice(32 * q, 32 * q + 32)
                        last = dve.tensor_tensor(sd[u][rows, :], ps[rows, 0:N], f32(sd[u][rows, :]), ALU.subtract)
                    last.then_inc(pj_read, 1)

            def invert(half, u):
                dve.wait_ge(exped, at(GAT_HEADS, half, u, GAT_HEADS))
                dve.reciprocal(recs[:, u, :, :], sums[:, u, :, :]).then_inc(inverted, 1)

            def divide(half, u, t):
                dve.wait_ge(inverted, at(1, half, u, 1))
                dve.wait_ge(back_made, at(NT, half, u, t + 1))
                dve.tensor_tensor(cx[:, t, :].rearrange("p (h e) -> p h e", e=GAT_DIM),
                                  back_bank[:, 0:D].rearrange("p (h e) -> p h e", e=GAT_DIM),
                                  recs[:, u, :, t].unsqueeze(2).to_broadcast([P, GAT_HEADS, GAT_DIM]), ALU.mult).then_inc(back_read, 1)

            def elu_argument(half, u):
                dve.wait_ge(ctx_bias, at(1, half, u, 1))
                dve.tensor_scalar(ce[:, :, :], cx[:, :, :], 0.0, None, ALU.min).then_inc(ctx_min, 1)

            def elu_and_gate(half, u):
                dve.wait_ge(ctx_exp, at(1, half, u, 1))
                dve.scalar_tensor_tensor(cx[:, :, :], ce[:, :, :], -1.0, cx[:, :, :], ALU.add, ALU.max).then_inc(elu_done, 1)
                dve.wait_ge(elu_done, at(1, half, u, 1))
                dve.wait_ge(ln_done, at(NT, half, u, 0))
                dve.scalar_tensor_tensor(mix[:, :, :], gate[u][:, :, :], 1.0, cx[:, :, :], ALU.add, ALU.mult).then_inc(gated, 1)

            def statistics(half, u):
                dve.wait_ge(summed, at(1, half, u, 1))
                for t in range(NT):
                    dve.bn_stats(stats[:, t, :], mix[:, t, :]).then_inc(bn, 1)
                for t in range(NT):
                    held(dve, bn, at(NT, half, u, t + 1), passed)
                    dve.bn_aggr(mv[:, t, :], stats[:, t, :]).then_inc(aggr, 1)

            def slot(cur, nxt, prev):
                for j in range(GAT_HEADS):
                    if cur:
                        held(dve, lrelu, at(GAT_HEADS, *cur, j + 1), passed)
                        for t in range(NT):
                            last = dve.tensor_tensor_reduce(
                                out=v_sb[:, j % 3, t, :], in0=z_ps[j % 2][:, t, :], in1=v_sb[:, j % 3, t, :], scale=-1.0,
                                scalar=BIG, op0=ALU.add, op1=ALU.min, accum_out=nmax[:, cur[1], j, t:t + 1])
                        last.then_inc(maxed, 1)
                    if prev and j - 1 in BACK_PLAN:
                        divide(*prev, BACK_PLAN[j - 1])
                    if prev and j == 9:
                        elu_and_gate(*prev)
                    if nxt and PLAN.get(j) in READ_STEPS:
                        lo_of_step(*nxt, PLAN[j])
                    if head := behind(cur, prev, GAT_HEADS, j, T_LAG):
                        half, u, h = head
                        dve.wait_ge(pt_hi_done, at(GAT_HEADS, half, u, h + 1))
                        dve.tensor_tensor(pt_lo[:, h % 3], pt_ps[h % 2][:, :, :], f32(pt_hi[:, h % 3]), ALU.subtract).then_inc(pt_split, 1)
                    if prev and j == 2:
                        invert(*prev)
                    if prev and j == 7:
                        elu_argument(*prev)
                    if prev and j == 11:
                        statistics(*prev)

            every_slot(dve, 0, slot)

        @block.tensor
        def _(pe):
            start(pe, pj_made, back_made, scores, transposed, contexts)

            def make_step(half, u, k, chunks):
                ps = pj_bank(k)
                if chunks[0] == 0:
                    if k == X:
                        pe.wait_ge(pj_read, reads(half, u, SD) - len(READ_STEPS))
                    elif k == TT:
                        pe.wait_ge(back_read, at(NT, half, u, -NT))
                        pe.wait_ge(pj_hi, at(len(HI_STEPS), half, u, HI_STEPS[H + 1]))
                    elif k in (X + 1, LAST):
                        pe.wait_ge(gate_done, at(NT, half, u, 0 if k == X + 1 else 1))
                    else:
                        pe.wait_ge(pj_read, reads(half, u, {H: X, H + 1: H, TT + 1: H + 1, G: TT, SD: TT + 1}[k]))
                if k in (X, X + 1):
                    t = k - X
                    pe.wait_ge(x_loaded[u], half * 32 + 32)
                    for c in chunks:
                        last = pe.transpose(ps[:, c * P:(c + 1) * P], x_sb[u][:, t, c * P:(c + 1) * P], ident[:, :])
                elif k in (H, H + 1, G, LAST):
                    m = 0 if k in (H, H + 1) else 1
                    t = 0 if k in (H, G) else 1
                    rows = slice(t * P, (t + 1) * P)
                    for c in chunks:
                        last = product(pe, ps[:, 0:D], (xt_hi[:, c, rows], xt_lo[:, c, rows]), (w_hi[:, m, c, :], w_lo[:, m, c, :]),
                                       first=c == 0, last=m == 0 and c == DC - 1)
                    if m == 1 and DC - 1 in chunks:
                        last = pe.matmul(ps[:, 0:D], ones[:, :], hb[:, :], start=False, stop=True)
                elif k in (TT, TT + 1):
                    t = k - TT
                    for c in chunks:
                        last = pe.transpose(ps[:, c * P:(c + 1) * P], th[:, t, c * P:(c + 1) * P], ident[:, :])
                else:
                    for c in chunks:
                        last = product(pe, ps[:, 0:N], (sd_hi[:, c, :], sd_lo[:, c, :]), (tt_hi[:, c, :], tt_lo[:, c, :]),
                                       first=c == 0, last=c == DC - 1)
                if DC - 1 in chunks:
                    last.then_inc(pj_made, 1)

            def make_back(half, u, t, cur, nxt):
                if t == 0:
                    pe.wait_ge(ctx_read, at(GROUPS, half, u, GROUPS))
                    if nxt:
                        pe.wait_ge(pj_read, reads(*nxt, X + 1))
                    else:
                        pe.wait_ge(gate_done, at(NT, *(cur or (half, u)), NT))
                else:
                    pe.wait_ge(back_read, at(NT, half, u, t))
                for c in range(GROUPS):
                    last = pe.matmul(back_bank[:, c * 2 * GAT_DIM:(c + 1) * 2 * GAT_DIM], ct[u][:, c, t * P:(t + 1) * P], fold[:, :], start=True, stop=True)
                last.then_inc(back_made, 1)

            def slot(cur, nxt, prev):
                for j in range(GAT_HEADS):
                    if cur:
                        half, u = cur
                        if j == 0:
                            pe.wait_ge(pj_read, reads(half, u, SD))
                            pe.wait_ge(mask_ready, at(1, half, u, 1))
                        pe.wait_ge(maxed, at(GAT_HEADS, half, u, j - 1))
                        for t in range(NT):
                            z = z_ps[j % 2][:, t, :]
                            pe.matmul(z, sel_dst[:, j, :], sd[u][:, :], start=True, stop=False)
                            pe.matmul(z, sd[u][:, t * P:(t + 1) * P], sel_src[:, j, :], start=False, stop=False)
                            last = pe.matmul(z, ident_bf[:, :], mask[u][:, t, :], start=False, stop=True)
                        last.then_inc(scores, 1)
                    for k, chunks in PE_PLAN[j] if nxt else ():
                        make_step(*nxt, k, chunks)
                    if head := behind(cur, prev, GAT_HEADS, j, T_LAG):
                        half, u, h = head
                        pe.wait_ge(exped, at(GAT_HEADS, half, u, h + 1))
                        pe.wait_ge(pt_split, at(GAT_HEADS, half, u, h - 1))
                        for t in range(NT):
                            for kt in range(NT):
                                last = pe.transpose(pt_ps[h % 2][:, kt, t * P:(t + 1) * P], exps[:, h % 4, t, kt * P:(kt + 1) * P], ident[:, :])
                        last.then_inc(transposed, 1)
                    if head := behind(cur, prev, GAT_HEADS, j, C_LAG):
                        half, u, h = head
                        c = h // 2
                        pe.wait_ge(pt_split, at(GAT_HEADS, half, u, h + 1))
                        if h % 2 == 0:
                            pe.wait_ge(ctx_read, at(GROUPS, half, u, c - 1))
                        for kt in range(NT):
                            for part in (pt_lo, pt_hi):
                                last = pe.matmul(cx_ps[c % 2][:, 0:N], h_split[u][:, kt, h, :], part[:, h % 3, kt, :],
                                                 start=h % 2 == 0 and kt == 0 and part is pt_lo,
                                                 stop=h % 2 == 1 and kt == NT - 1 and part is pt_hi)
                        last.then_inc(contexts, 1)
                    if prev and j in BACK_PLAN:
                        make_back(*prev, BACK_PLAN[j], cur, nxt)

            pe.wait_ge(consts_loaded, 7 * 16)
            pe.wait_ge(consts_ready, 1)
            pe.wait_ge(w_split, 4)
            pe.wait_ge(hb_ready, 1)
            every_slot(pe, 0, slot)


def attention_phase(nc, y, adj, w, b_col, b_row, ident_dram, w_stage, w_loaded):
    STEPS = 7
    Q, K, V, O = range(4)
    with ExitStack() as ctx:
        def sb(name, shape, dt=F32):
            return ctx.enter_context(nc.sbuf_tensor("a_" + name, shape, dt))

        def sem(name):
            return ctx.enter_context(nc.semaphore("a_" + name))

        x_sb = [sb(f"x{p}", [P, NT, D]) for p in range(2)]
        adj_sb = [sb(f"adj{p}", [P, NT, N], U8) for p in range(2)]
        mask = [sb(f"mask{p}", [P, NT, N]) for p in range(2)]
        w_hi, w_lo = sb("w_hi", [P, 4, DC, D], F32R), sb("w_lo", [P, 4, DC, D], F32R)
        bc_stage, br_stage = sb("bc_stage", [P, 3, DC]), sb("br_stage", [P, D])
        bc, br = sb("bc", [P, 3, DC]), sb("br", [P, D])
        ident = sb("ident", [P, P])
        half_neg = sb("half_neg", [P, NT])
        xt_hi, xt_lo = sb("xt_hi", [P, DC, N], F32R), sb("xt_lo", [P, DC, N], F32R)
        qk_hi = [sb(f"qk_hi{p}", [P, DC, 2, N], F32R) for p in range(2)]
        qk_lo = [sb(f"qk_lo{p}", [P, DC, 2, N], F32R) for p in range(2)]
        v = sb("v", [P, NT, D])
        v_split_sb = [sb(f"v_split{p}", [P, NT, HEADS, P], F32R) for p in range(2)]
        logits = sb("logits", [P, 2, NT, N])
        probs = sb("probs", [P, 4, NT, N])
        nmax = sb("nmax", [P, 2, HEADS, NT])
        sums = sb("sums", [P, 2, HEADS, NT])
        recs = sb("recs", [P, 2, HEADS, NT])
        pt_hi, pt_lo = sb("pt_hi", [P, 2, NT, N], F32R), sb("pt_lo", [P, 2, NT, N], F32R)
        moved = sb("moved", [P, N])
        ct = sb("ct", [P, N])
        ct_hi, ct_lo = sb("ct_hi", [P, DC, N], F32R), sb("ct_lo", [P, DC, N], F32R)
        residual = [sb(f"residual{p}", [P, NT, D]) for p in range(2)]
        mix = sb("mix", [P, NT, D])
        stats = sb("stats", [P, NT, 6])
        mv = sb("mv", [P, NT, 2])
        var = sb("var", [P, NT])
        rstd = sb("rstd", [P, NT])
        out_sb = [sb(f"out{p}", [P, NT, D]) for p in range(2)]
        s_ps = [ctx.enter_context(nc.psum_tensor(f"a_s{i}", [P, NT, N], F32)) for i in range(2)]
        pt_ps = [ctx.enter_context(nc.psum_tensor(f"a_pt{i}", [P, NT, N], F32)) for i in range(2)]
        cx_ps = [ctx.enter_context(nc.psum_tensor(f"a_cx{i}", [P, 512], F32)) for i in range(2)]
        pj_ps = [ctx.enter_context(nc.psum_tensor(f"a_pj{i}", [P, 512], F32)) for i in range(2)]

        passed = sem("passed")
        x_loaded = [sem(f"x_loaded{p}") for p in range(2)]
        stored = [sem(f"stored{p}") for p in range(2)]
        ident_loaded, bias_loaded = sem("ident_loaded"), sem("bias_loaded")
        half_ready = sem("half_ready")
        w_hi_done, w_split, b_ready = sem("w_hi_done"), sem("w_split"), sem("b_ready")
        mask_ready, x_biased = sem("mask_ready"), sem("x_biased")
        pj_made = sem("pj_made")
        pj_hi = sem("pj_hi")
        pj_read = sem("pj_read")
        v_read = sem("v_read")
        back_made, back_read = sem("back_made"), sem("back_read")
        v_hi_done, v_split = sem("v_hi_done"), sem("v_split")
        scores, maxed, exped = sem("scores"), sem("maxed"), sem("exped")
        inverted, normed = sem("inverted"), sem("normed")
        transposed, pt_hi_done, pt_split = sem("transposed"), sem("pt_hi_done"), sem("pt_split")
        contexts, ct_moved, ct_added = sem("contexts"), sem("ct_moved"), sem("ct_added")
        ct_hi_done, ct_split = sem("ct_hi_done"), sem("ct_split")
        bn, aggr, var_eps, rstd_done, ln_done = sem("bn"), sem("aggr"), sem("var_eps"), sem("rstd_done"), sem("ln_done")

        X, C, VS = 0, 2, 5
        HI_STEPS = VS
        BACK_AT = VS + 1
        PLAN = {0: X, 2: C + 1, 3: C + 2, 4: VS}
        LATE_PLAN = {0: X + 1, 1: C, 5: VS + 1}
        BACK_PLAN, LATE_BACK_PLAN = {5: 1}, {4: 0}
        T_LAG, C_LAG = 2, 3

        def step(half, u, k):
            return at(STEPS, half, u, k)

        def pj_bank(u, k):
            return pj_ps[(u + 1 + k) % 2]

        def back_bank(u, t):
            return pj_ps[(u + 1 + BACK_AT + t) % 2]

        def v_parts(u, t, s):
            return [v_split_sb[u][:, t, s::2, half * HEAD_DIM:(half + 1) * HEAD_DIM] for half in (s, 1 - s)]

        def rows_of(s):
            return slice(s * HEAD_DIM, (s + 1) * HEAD_DIM)

        def samples(half, u):
            return y[bass.ds(half * 2 + u, 1), :, :].rearrange("o (t p) d -> p (o t) d", p=P)

        block = ctx.enter_context(nc.Block())

        def layers(eng, begin, slot):
            with eng.Fori(0, LAYERS) as layer:
                begin(layer)
                every_slot(eng, layer * HALVES, slot)

        @block.sync
        def _(sp):
            def load(pair, u):
                sp.dma_start(x_sb[u][:, :, :], samples(pair, u)).then_inc(x_loaded[u], 16)
                sp.dma_start(adj_sb[u][:, :, :], adj[bass.ds(pair * 2 + u, 1), :, :].rearrange("o (t p) d -> p (o t) d", p=P)).then_inc(x_loaded[u], 16)

            def load_biases(layer):
                sp.dma_start(bc_stage[:, :, :], b_col[bass.ds(layer, 1), :, :].rearrange("o p n -> p (o n)").rearrange("p (m c) -> p m c", m=3)).then_inc(bias_loaded, 16)
                sp.dma_start(br_stage[:, :], b_row[bass.ds(layer, 1), :].rearrange("o n -> (o n)").partition_broadcast(P)).then_inc(bias_loaded, 16)

            def store(half, pair, u):
                held(sp, ln_done, at(NT, half, u, NT), passed)
                sp.dma_start(samples(pair, u), out_sb[u][:, :, :]).then_inc(stored[u], 16)

            def load_again(half, u, pair):
                held(sp, x_biased, at(1, half, u, 1), passed)
                load(pair, u)

            def layer_samples(layer, more):
                first = layer * HALVES
                for u in range(2):
                    load_again(first, u, 1)
                with sp.Fori(0, HALVES - 2) as pair:
                    for u in range(2):
                        load_again(first + pair + 1, u, pair + 2)
                        store(first + pair, pair, u)
                for u in range(2):
                    if more:
                        load_again(first + (HALVES - 1), u, 0)
                    store(first + (HALVES - 2), HALVES - 2, u)
                for u in range(2):
                    store(first + (HALVES - 1), HALVES - 1, u)

            start(sp, *stored)
            sp.dma_start(ident[:, :], ident_dram).then_inc(ident_loaded, 16)
            load(0, 0)
            load_biases(0)
            load(0, 1)
            with sp.Fori(0, LAYERS - 1) as layer:
                held(sp, w_split, layer * 4 + 4, passed)
                held(sp, b_ready, layer + 1, passed)
                load_biases(layer + 1)
                load_att_weights(sp, w, layer + 1, w_stage, w_loaded)
                layer_samples(layer, True)
            layer_samples(LAYERS - 1, False)
            for u in range(2):
                sp.wait_ge(stored[u], 16 * HALVES * LAYERS + START)

        @block.gpsimd
        def _(pool):
            start(pool, mask_ready, x_biased, v_split, rstd_done, var_eps, ln_done)
            pool.memset(half_neg[:, :], -0.5).then_inc(half_ready, 1)
            pool.wait_ge(half_ready, 1)

            def make_mask(half, u, prev):
                if prev:
                    pool.wait_ge(maxed, at(HEADS, *prev, HEADS))
                held(pool, x_loaded[u], half * 32 + 32, passed)
                pool.tensor_scalar(mask[u][:, :, :], adj_sb[u][:, :, :], -1.0, -NEG * HEAD_DIM ** 0.5, ALU.add, ALU.mult).then_inc(mask_ready, 1)

            def add_output_bias(half, u):
                pool.wait_ge(pj_made, step(half, u, C))
                pool.wait_ge(back_read, at(NT, half, u, -NT))
                for t in range(NT):
                    last = pool.tensor_tensor(residual[u][:, t, :], x_sb[u][:, t, :], br[:, :], ALU.add)
                last.then_inc(x_biased, 1)

            def low_v(half, u, t):
                pool.wait_ge(v_hi_done, at(NT, half, u, t + 1))
                src = v[:, t, :].rearrange("p (h two d) -> p h two d", two=2, d=HEAD_DIM)
                for s in range(2):
                    hi, lo = v_parts(u, t, s)
                    last = pool.tensor_tensor(lo, src[:, :, s, :], f32(hi), ALU.subtract)
                last.then_inc(v_split, 1)

            def inverse_std(half, u, eps):
                held(pool, aggr, at(NT, half, u, NT), passed)
                pool.tensor_scalar(var[:, :], mv[:, :, 1], eps, None, ALU.add).then_inc(var_eps, 1)
                pool.wait_ge(var_eps, at(1, half, u, 1))
                pool.tensor_tensor(rstd[:, :], var[:, :], half_neg[:, :], ALU.pow).then_inc(rstd_done, 1)

            def layer_norm(half, u):
                pool.wait_ge(stored[u], half * 16 + START)
                held(pool, rstd_done, at(1, half, u, 1), passed)
                for t in range(NT):
                    pool.tensor_scalar(out_sb[u][:, t, :], mix[:, t, :], mv[:, t, 0:1], rstd[:, t:t + 1], ALU.subtract, ALU.mult).then_inc(ln_done, 1)

            def begin(layer):
                pool.wait_ge(b_ready, layer + 1)

            def slot(cur, nxt, prev):
                for j in range(HEADS):
                    if cur and j == 0:
                        low_v(*cur, 1)
                    if nxt and j == 0:
                        make_mask(*nxt, prev)
                    if nxt and j == 5:
                        add_output_bias(*nxt)
                        low_v(*nxt, 0)
                    if prev and j == 5:
                        inverse_std(*prev, EPS)
                        layer_norm(*prev)

            layers(pool, begin, slot)

        @block.scalar
        def _(act):
            start(act, pj_hi, v_read, v_hi_done, exped, pt_hi_done, ct_moved, ct_hi_done)
            def copy_v(half, u, t):
                act.wait_ge(pj_made, step(half, u, VS + t) + 1)
                act.wait_ge(v_split, at(NT, half, u, 0))
                act.activation(v[:, t, :], pj_bank(u, VS + t)[:, 0:D], ACT.Identity).then_inc(v_read, 1)

            def hi_of_v(half, u, t):
                act.wait_ge(v_read, at(NT, half, u, t + 1))
                src = v[:, t, :].rearrange("p (h two d) -> p h two d", two=2, d=HEAD_DIM)
                for s in range(2):
                    last = act.activation(v_parts(u, t, s)[0], src[:, :, s, :], ACT.Identity)
                last.then_inc(v_hi_done, 1)

            def hi_of_step(half, u, k):
                ps = pj_bank(u, k)
                act.wait_ge(pj_made, step(half, u, k) + 1)
                if k < C:
                    cols = slice((k - X) * P, (k - X + 1) * P)
                    act.activation(xt_hi[:, :, cols], ps[:, 0:D].rearrange("p (c n) -> p c n", c=DC), ACT.Identity).then_inc(pj_hi, 1)
                else:
                    c = k - C
                    for m in (Q, K):
                        last = act.activation(qk_hi[u][:, c, m, :], ps[:, m * N:(m + 1) * N], ACT.Identity, bias=bc[:, m, c:c + 1])
                    last.then_inc(pj_hi, 1)

            def begin(layer):
                act.wait_ge(w_loaded, layer * 16 + 16)
                act.wait_ge(back_made, layer * (NT * B) + START)
                for m in range(4):
                    act.activation(w_hi[:, m], w_stage[:, m], ACT.Identity).then_inc(w_hi_done, 1)
                act.wait_ge(b_ready, layer + 1)

            def slot(cur, nxt, prev):
                for j in range(HEADS):
                    if nxt and j - 1 in LATE_PLAN:
                        hi_of_step(*nxt, LATE_PLAN[j - 1])
                    if head := behind(cur, prev, HEADS, j, 1):
                        half, u, h = head
                        i = (HEADS * u + h) % 4
                        act.wait_ge(maxed, at(HEADS, half, u, h + 1))
                        act.wait_ge(transposed, at(HEADS, half, u, h - 3))
                        for t in range(NT):
                            last = act.activation(probs[:, i, t, :], logits[:, h % 2, t, :], ACT.Exp, scale=-1.0,
                                                  bias=nmax[:, u, h, t:t + 1], accum_out=sums[:, u, h, t:t + 1])
                        last.then_inc(exped, 1)
                    if cur and j == 0:
                        copy_v(*cur, 1)
                    if nxt and j in PLAN and PLAN[j] < VS:
                        hi_of_step(*nxt, PLAN[j])
                    if head := behind(cur, prev, HEADS, j, T_LAG):
                        half, u, h = head
                        act.wait_ge(transposed, at(HEADS, half, u, h + 1))
                        act.wait_ge(contexts, at(HEADS, half, u, h - 1))
                        act.activation(pt_hi[:, h % 2], pt_ps[h % 2][:, :, :], ACT.Identity).then_inc(pt_hi_done, 1)
                    head = behind(cur, prev, HEADS, j, C_LAG + 1)
                    if head and head[2] % 2 == 1:
                        half, u, h = head
                        c = h // 2
                        act.wait_ge(ct_added, at(DC, half, u, c + 1))
                        act.wait_ge(back_made, at(NT, half, u, 0))
                        act.activation(ct_hi[:, c, :], ct[:, :], ACT.Identity, bias=bc[:, V, c:c + 1]).then_inc(ct_hi_done, 1)
                    head = behind(cur, prev, HEADS, j, C_LAG)
                    if head and head[2] % 2 == 1:
                        half, u, h = head
                        c = h // 2
                        act.wait_ge(contexts, at(HEADS, half, u, h + 1))
                        act.wait_ge(ct_added, at(DC, half, u, c))
                        for s in range(2):
                            last = act.activation(moved[rows_of(s), :], cx_ps[(3 * u + c) % 2][rows_of(1 - s), s * N:(s + 1) * N], ACT.Identity)
                        last.then_inc(ct_moved, 1)
                    if cur and j == 0:
                        hi_of_v(*cur, 1)
                    if nxt and PLAN.get(j) == VS:
                        copy_v(*nxt, 0)
                        hi_of_v(*nxt, 0)

            layers(act, begin, slot)

        @block.vector
        def _(dve):
            start(dve, pj_read, back_read, maxed, inverted, normed, pt_split, ct_added, ct_split, bn, aggr)

            def lo_of_step(half, u, k):
                ps = pj_bank(u, k)
                dve.wait_ge(pj_hi, at(HI_STEPS, half, u, k + 1))
                if k < C:
                    cols = slice((k - X) * P, (k - X + 1) * P)
                    dve.tensor_tensor(xt_lo[:, :, cols], ps[:, 0:D].rearrange("p (c n) -> p c n", c=DC), f32(xt_hi[:, :, cols]), ALU.subtract).then_inc(pj_read, 1)
                else:
                    c = k - C
                    for m in (Q, K):
                        last = dve.scalar_tensor_tensor(qk_lo[u][:, c, m, :], ps[:, m * N:(m + 1) * N], bc[:, m, c:c + 1],
                                                        f32(qk_hi[u][:, c, m, :]), ALU.add, ALU.subtract)
                    last.then_inc(pj_read, 1)

            def normalise(half, u, h):
                dve.wait_ge(exped, at(HEADS, half, u, h + 1))
                dve.reciprocal(recs[:, u, h, :], sums[:, u, h, :]).then_inc(inverted, 1)
                dve.wait_ge(inverted, at(HEADS, half, u, h + 1))
                for t in range(NT):
                    last = dve.tensor_scalar(probs[:, (HEADS * u + h) % 4, t, :], probs[:, (HEADS * u + h) % 4, t, :], recs[:, u, h, t:t + 1], None, ALU.mult)
                last.then_inc(normed, 1)

            def begin(layer):
                dve.wait_ge(w_loaded, layer * 16 + 16)
                dve.wait_ge(bias_loaded, layer * 32 + 32)
                dve.wait_ge(x_biased, layer * B + START)
                dve.wait_ge(ct_hi_done, layer * (DC * B) + START)
                dve.wait_ge(ct_split, layer * (DC * B) + START)
                dve.tensor_copy(bc[:, :, :], bc_stage[:, :, :])
                dve.tensor_copy(br[:, :], br_stage[:, :]).then_inc(b_ready, 1)
                dve.wait_ge(b_ready, layer + 1)
                for m in range(4):
                    dve.wait_ge(w_hi_done, layer * 4 + m + 1)
                    dve.tensor_tensor(w_lo[:, m], w_stage[:, m], f32(w_hi[:, m]), ALU.subtract).then_inc(w_split, 1)

            def add_back(half, u, t):
                dve.wait_ge(x_biased, at(1, half, u, 1))
                dve.wait_ge(ln_done, at(NT, half, u, 0))
                dve.wait_ge(back_made, at(NT, half, u, t + 1))
                dve.tensor_tensor(mix[:, t, :], back_bank(u, t)[:, 0:D], residual[u][:, t, :], ALU.add).then_inc(back_read, 1)

            def statistics(half, u):
                for t in range(NT):
                    dve.wait_ge(back_read, at(NT, half, u, t + 1))
                    dve.bn_stats(stats[:, t, :], mix[:, t, :]).then_inc(bn, 1)
                for t in range(NT):
                    held(dve, bn, at(NT, half, u, t + 1), passed)
                    dve.bn_aggr(mv[:, t, :], stats[:, t, :]).then_inc(aggr, 1)

            def slot(cur, nxt, prev):
                for j in range(HEADS):
                    if nxt and LATE_PLAN.get(j - 1) == X + 1:
                        lo_of_step(*nxt, X + 1)
                    if cur:
                        half, u = cur
                        if j == 0:
                            dve.wait_ge(mask_ready, at(1, half, u, 1))
                        dve.wait_ge(scores, at(HEADS, half, u, j + 1))
                        held(dve, exped, at(HEADS, half, u, j - 1), passed)
                        for t in range(NT):
                            last = dve.tensor_tensor_reduce(
                                out=logits[:, j % 2, t, :], in0=s_ps[j % 2][:, t, :], in1=mask[u][:, t, :], scale=-HEAD_DIM ** -0.5,
                                scalar=BIG, op0=ALU.add, op1=ALU.min, accum_out=nmax[:, u, j, t:t + 1])
                        last.then_inc(maxed, 1)
                    if nxt and LATE_PLAN.get(j - 1) == C:
                        lo_of_step(*nxt, LATE_PLAN[j - 1])
                    if prev and j - 1 in LATE_BACK_PLAN:
                        add_back(*prev, LATE_BACK_PLAN[j - 1])
                    if head := behind(cur, prev, HEADS, j, 1):
                        normalise(*head)
                    pair = behind(cur, prev, HEADS, j, C_LAG + 1)
                    pair = pair if pair and pair[2] % 2 == 1 else None
                    if pair:
                        half, u, h = pair
                        c = h // 2
                        dve.wait_ge(ct_moved, at(DC, half, u, c + 1))
                        dve.wait_ge(ct_split, at(DC, half, u, c))
                        for s in range(2):
                            rows = rows_of(s)
                            last = dve.tensor_tensor(ct[rows, :], cx_ps[(3 * u + c) % 2][rows, s * N:(s + 1) * N], moved[rows, :], ALU.add)
                        last.then_inc(ct_added, 1)
                    if nxt and PLAN.get(j, VS) < VS:
                        lo_of_step(*nxt, PLAN[j])
                    if prev and j in BACK_PLAN:
                        add_back(*prev, BACK_PLAN[j])
                    if head := behind(cur, prev, HEADS, j, T_LAG):
                        half, u, h = head
                        dve.wait_ge(pt_hi_done, at(HEADS, half, u, h + 1))
                        dve.tensor_tensor(pt_lo[:, h % 2], pt_ps[h % 2][:, :, :], f32(pt_hi[:, h % 2]), ALU.subtract).then_inc(pt_split, 1)
                    if pair:
                        half, u, h = pair
                        c = h // 2
                        dve.wait_ge(ct_hi_done, at(DC, half, u, c + 1))
                        dve.scalar_tensor_tensor(ct_lo[:, c, :], ct[:, :], bc[:, V, c:c + 1], f32(ct_hi[:, c, :]), ALU.add, ALU.subtract).then_inc(ct_split, 1)
                    if prev and j == 5:
                        statistics(*prev)

            layers(dve, begin, slot)

        @block.tensor
        def _(pe):
            def make_step(half, u, k, prev):
                ps = pj_bank(u, k)
                if k in (X, X + 1):
                    pe.wait_ge(v_read, at(NT, half, u, k - X - 1))
                    if k == X and prev:
                        pe.wait_ge(back_read, at(NT, *prev, 0))
                else:
                    pe.wait_ge(pj_read, at(HI_STEPS, half, u, k if k == C else k - 1))
                    if k == BACK_AT:
                        pe.wait_ge(back_read, at(NT, half, u, -3))
                if k < C:
                    t = k - X
                    pe.wait_ge(x_loaded[u], half * 32 + 32)
                    for c in range(DC):
                        last = pe.transpose(ps[:, c * P:(c + 1) * P], x_sb[u][:, t, c * P:(c + 1) * P], ident[:, :])
                elif k < VS:
                    cols = slice((k - C) * P, (k - C + 1) * P)
                    for m in (Q, K):
                        for c in range(DC):
                            last = product(pe, ps[:, m * N:(m + 1) * N], (w_hi[:, m, c, cols], w_lo[:, m, c, cols]), (xt_hi[:, c, :], xt_lo[:, c, :]),
                                           first=c == 0, last=c == DC - 1)
                else:
                    rows = slice((k - VS) * P, (k - VS + 1) * P)
                    for c in range(DC):
                        last = product(pe, ps[:, 0:D], (xt_hi[:, c, rows], xt_lo[:, c, rows]), (w_hi[:, V, c, :], w_lo[:, V, c, :]),
                                       first=c == 0, last=c == DC - 1)
                last.then_inc(pj_made, 1)

            def make_back(half, u, t, cur, nxt):
                if t == 0:
                    pe.wait_ge(ct_split, at(DC, half, u, DC))
                if nxt:
                    pe.wait_ge(pj_read, at(HI_STEPS, *nxt, HI_STEPS))
                    pe.wait_ge(v_read, at(NT, *nxt, t))
                else:
                    pe.wait_ge(v_read, at(NT, *(cur or (half, u)), NT))
                    pe.wait_ge(back_read, at(NT, half, u, 0))
                rows = slice(t * P, (t + 1) * P)
                for c in range(DC):
                    last = product(pe, back_bank(u, t)[:, 0:D], (ct_hi[:, c, rows], ct_lo[:, c, rows]), (w_hi[:, O, c, :], w_lo[:, O, c, :]),
                                   first=c == 0, last=c == DC - 1)
                last.then_inc(back_made, 1)

            def begin(layer):
                pe.wait_ge(w_split, layer * 4 + 4)
                pe.wait_ge(back_read, layer * (NT * B) + START)

            def slot(cur, nxt, prev):
                for j in range(HEADS):
                    if cur:
                        half, u = cur
                        if j == 0:
                            pe.wait_ge(pj_read, at(HI_STEPS, half, u, HI_STEPS))
                        pe.wait_ge(maxed, at(HEADS, half, u, j - 1))
                        c, rows = j // 2, rows_of(j % 2)
                        for t in range(NT):
                            nodes = slice(t * P, (t + 1) * P)
                            last = product(pe, s_ps[j % 2][:, t, :], (qk_hi[u][rows, c, Q, nodes], qk_lo[u][rows, c, Q, nodes]),
                                           (qk_hi[u][rows, c, K, :], qk_lo[u][rows, c, K, :]))
                        last.then_inc(scores, 1)
                    if nxt and j in PLAN:
                        make_step(*nxt, PLAN[j], prev)
                    if prev and j in BACK_PLAN:
                        make_back(*prev, BACK_PLAN[j], cur, nxt)
                    if head := behind(cur, prev, HEADS, j, T_LAG):
                        half, u, h = head
                        i = (HEADS * u + h) % 4
                        pe.wait_ge(normed, at(HEADS, half, u, h + 1))
                        pe.wait_ge(pt_split, at(HEADS, half, u, h - 1))
                        for t in range(NT):
                            for kt in range(NT):
                                last = pe.transpose(pt_ps[h % 2][:, kt, t * P:(t + 1) * P], probs[:, i, t, kt * P:(kt + 1) * P], ident[:, :])
                        last.then_inc(transposed, 1)
                    if head := behind(cur, prev, HEADS, j, C_LAG):
                        half, u, h = head
                        c = h // 2
                        pe.wait_ge(pt_split, at(HEADS, half, u, h + 1))
                        if h == 0:
                            pe.wait_ge(v_split, at(NT, half, u, NT))
                        if h % 2 == 0:
                            pe.wait_ge(ct_added, at(DC, half, u, c - 1))
                        cols = slice(h % 2 * N, (h % 2 + 1) * N)
                        for kt in range(NT):
                            for part in (pt_lo, pt_hi):
                                last = pe.matmul(cx_ps[(3 * u + c) % 2][:, cols], v_split_sb[u][:, kt, h, :], part[:, h % 2, kt, :],
                                                 start=kt == 0 and part is pt_lo, stop=kt == NT - 1 and part is pt_hi)
                        last.then_inc(contexts, 1)
                    if nxt and j in LATE_PLAN:
                        make_step(*nxt, LATE_PLAN[j], prev)
                    if prev and j in LATE_BACK_PLAN:
                        make_back(*prev, LATE_BACK_PLAN[j], cur, nxt)

            start(pe, pj_made, back_made, scores, transposed, contexts)
            pe.wait_ge(ident_loaded, 16)
            layers(pe, begin, slot)


def load_att_weights(sp, w, layer, w_stage, w_loaded):
    sp.dma_start(w_stage[:, :, :, :], w[bass.ds(layer, 1), :, :].rearrange("o p n -> p (o n)").rearrange("p (m c n) -> p m c n", m=4, c=DC)).then_inc(w_loaded, 16)


def build(nc, x, adj, gat_w, gat_sd, gat_b, gat_hb, att_w, att_b_col, att_b_row, ident, sel, fold, y):
    with ExitStack() as ctx:
        w_stage = ctx.enter_context(nc.sbuf_tensor("w_stage", [P, 4, DC, D], F32))
        w_loaded = ctx.enter_context(nc.semaphore("w_loaded"))
        gat_phase(nc, x, adj, y, gat_w, gat_sd, gat_b, gat_hb, ident, sel, fold, att_w, w_stage, w_loaded)
        attention_phase(nc, y, adj, att_w, att_b_col, att_b_row, ident, w_stage, w_loaded)


def kernel(**inputs):
    import numpy as np
    import concourse.bacc as bacc
    from concourse.bass_utils import run_bass_kernel_spmd

    a = {name: np.asarray(value) for name, value in inputs.items()}

    def rows_in(mats):
        return np.ascontiguousarray(np.stack([m.reshape(DC, P, -1) for m in mats]).transpose(2, 0, 1, 3))

    w_heads = a["L0_gnn_W"].transpose(1, 0, 2).reshape(D, D)
    w_sd = np.zeros((D, P), np.float32)
    for h in range(GAT_HEADS):
        rows = slice(h * GAT_DIM, (h + 1) * GAT_DIM)
        for q, name in enumerate(("L0_gnn_w_dst", "L0_gnn_w_dst", "L0_gnn_w_src", "L0_gnn_w_src")):
            w_sd[rows, 32 * q + h] = a[name][h, :, 0]
    sel = np.zeros((P, 2, GAT_HEADS), np.float32)
    for h in range(GAT_HEADS):
        for q in range(4):
            sel[32 * q + h, q // 2, h] = 1.0
    names = [f"L{layer}_gnn_" for layer in range(1, LAYERS + 1)]
    arrays = {
        "x": np.ascontiguousarray(a["x"]),
        "adj": np.ascontiguousarray(a["adj"]),
        "gat_w": rows_in([w_heads, a["L0_gnn_H_w"].T]),
        "gat_sd": rows_in([w_sd])[:, 0],
        "gat_b": np.tile(a["L0_gnn_b"], GAT_HEADS),
        "gat_hb": np.concatenate([np.tile(np.concatenate([a["L0_gnn_H_b"][None], np.zeros((31, D), np.float32)]), (2, 1))]),
        "att_w": np.stack([rows_in([a[n + m] for m in ("Wq", "Wk", "Wv", "Wf")]).reshape(P, -1) for n in names]),
        "att_b_col": np.stack([rows_in([a[n + m].reshape(D, 1) for m in ("bq", "bk", "bv")]).reshape(P, -1) for n in names]),
        "att_b_row": np.stack([a[n + "bf"] for n in names]),
        "ident": np.eye(P, dtype=np.float32),
        "sel": sel,
        "fold": np.kron(np.eye(2), np.tile(np.eye(GAT_DIM), (2, 1))).astype(np.float32),
    }
    arrays = {n: np.ascontiguousarray(v) for n, v in arrays.items()}
    nc = bacc.Bacc("TRN2", target_bir_lowering=False, num_devices=1)
    drams = [nc.dram_tensor(n, v.shape, mybir.dt.from_np(v.dtype), kind="ExternalInput").ap() for n, v in arrays.items()]
    y = nc.dram_tensor("y", (B, N, D), F32, kind="ExternalOutput").ap()
    build(nc, *drams, y)
    return run_bass_kernel_spmd(nc, [arrays], core_ids=[0]).results[0]["y"]
```
